# Optimizing a Trainium2 kernel written in Bass

```python
import numpy as np
import jax
import jax.numpy as jnp

def _softmax(x, axis=-1):
    return jax.nn.softmax(x, axis=axis)

def _gelu(x):
    return jax.nn.gelu(x, approximate=True)

def _silu(x):
    return jax.nn.silu(x)

def _sigmoid(x):
    return jax.nn.sigmoid(x)

def _layernorm(x, axis=-1, eps=1e-05):
    m = jnp.mean(x, axis=axis, keepdims=True)
    v = jnp.var(x, axis=axis, keepdims=True)
    return (x - m) / jnp.sqrt(v + eps)

def _scatter_add(tgt, idx, src, axis=0):
    return tgt.at[idx].add(src)

def _segment_sum(src, seg, n):
    return jax.ops.segment_sum(src, seg, n)
kernel_name = 'mk_gnn_preln_d4_gnn_r16_0a44e4'

def setup_inputs(seed: int=0):
    np.random.seed(seed)
    _w = jnp.asarray

    def _rec_inputs():
        import jax
        import jax.numpy as jnp
        _gk = jax.random.key(seed)
        x = -0.000202 + 1 * jax.random.normal(jax.random.fold_in(_gk, 1), (6250, 128), jnp.float32)
        src = jax.random.randint(jax.random.fold_in(_gk, 2), (200000,), 0, 6250, jnp.int32)
        dst = jnp.minimum((6250 * jax.random.uniform(jax.random.fold_in(_gk, 3), (200000,)) ** 2.0).astype(jnp.int32), 99999)
        _o = jnp.argsort(dst, stable=True)
        src = src[_o]
        dst = dst[_o]
        edge_type_8 = jax.random.randint(jax.random.fold_in(_gk, 13), (200000,), 0, 8, jnp.int32)
        edge_weight1 = jax.random.uniform(jax.random.fold_in(_gk, 14), (200000, 1), jnp.float32, 0.0, 0.999999)
        return (x, src, dst, edge_type_8, edge_weight1)
    x, src, dst, edge_type_8, edge_weight1 = _rec_inputs()

    def _L0_gnn_setup():
        import jax, jax.numpy as jnp
        import numpy as np
        N_NODES = 3125
        IN_CH = 128
        OUT_CH = 128
        N_EDGES = 40000
        key = jax.random.key(seed)
        k1, k2, k3, k4 = jax.random.split(key, 4)
        x = jax.random.normal(k1, (N_NODES, IN_CH), dtype=jnp.float32)
        edge_index = jax.random.randint(k2, (2, N_EDGES), 0, N_NODES, dtype=jnp.int64)
        bound = 1.0 / np.sqrt(2 * IN_CH)
        W = jax.random.uniform(k3, (OUT_CH, 2 * IN_CH), minval=-bound, maxval=bound, dtype=jnp.float32)
        b = jax.random.uniform(k4, (OUT_CH,), minval=-bound, maxval=bound, dtype=jnp.float32)
        return {'x': x, 'edge_index': edge_index, 'W': W, 'b': b}
    _L0_gnn_all = _L0_gnn_setup()
    _L0_gnn_in = {k: v for k, v in _L0_gnn_all.items() if k in ('W', 'b')}
    del _L0_gnn_all

    def _L1_gnn_setup():
        import jax, jax.numpy as jnp
        import numpy as np
        N_NODES = 3125
        N_EDGES = 50000
        IN_FEAT = 128
        OUT_FEAT = 128
        key = jax.random.key(seed)
        ks = jax.random.split(key, 9)
        s = 1.0 / np.sqrt(IN_FEAT)
        return {'x': jax.random.normal(ks[0], (N_NODES, IN_FEAT), dtype=jnp.float32), 'src': jax.random.randint(ks[1], (N_EDGES,), 0, N_NODES), 'dst': jax.random.randint(ks[2], (N_EDGES,), 0, N_NODES), 'W1': jax.random.uniform(ks[3], (IN_FEAT, OUT_FEAT), jnp.float32, -s, s), 'b1': jax.random.uniform(ks[4], (OUT_FEAT,), jnp.float32, -s, s), 'W2': jax.random.uniform(ks[5], (OUT_FEAT, 1), jnp.float32, -s, s), 'b2': jax.random.uniform(ks[6], (1,), jnp.float32, -s, s), 'W4': jax.random.uniform(ks[7], (IN_FEAT, OUT_FEAT), jnp.float32, -s, s), 'b4': jax.random.uniform(ks[8], (OUT_FEAT,), jnp.float32, -s, s)}
    _L1_gnn_all = _L1_gnn_setup()
    _L1_gnn_in = {k: v for k, v in _L1_gnn_all.items() if k in ('W1', 'b1', 'W2', 'b2', 'W4', 'b4')}
    del _L1_gnn_all

    def _L2_gnn_setup():
        import jax, jax.numpy as jnp
        import numpy as np
        N = 3125
        E = 50000
        D = 128
        EPS = 1e-12
        key = jax.random.key(seed)
        ks = jax.random.split(key, 8)
        x = jax.random.normal(ks[0], (N, D), dtype=jnp.float32)
        edge_index = jax.random.randint(ks[1], (2, E), 0, N, dtype=jnp.int64)
        s = 1.0 / np.sqrt(D)
        Wp = jax.random.uniform(ks[2], (D, D), jnp.float32, -s, s)
        bp = jax.random.uniform(ks[3], (D,), jnp.float32, -s, s)
        Wl = jax.random.uniform(ks[4], (D, D), jnp.float32, -s, s)
        bl = jax.random.uniform(ks[5], (D,), jnp.float32, -s, s)
        Wr = jax.random.uniform(ks[6], (D, D), jnp.float32, -s, s)
        return {'x': x, 'edge_index': edge_index, 'Wp': Wp, 'bp': bp, 'Wl': Wl, 'bl': bl, 'Wr': Wr}
    _L2_gnn_all = _L2_gnn_setup()
    _L2_gnn_in = {k: v for k, v in _L2_gnn_all.items() if k in ('Wp', 'bp', 'Wl', 'bl', 'Wr')}
    del _L2_gnn_all

    def _L3_gnn_setup():
        import jax, jax.numpy as jnp
        import numpy as np
        N_NODES = 625
        N_EDGES = 40000
        IN_FEAT = 128
        OUT_FEAT = 128
        NUM_RELS = 8
        key = jax.random.key(seed)
        ks = jax.random.split(key, 7)
        feat = jax.random.normal(ks[0], (N_NODES, IN_FEAT), dtype=jnp.float32)
        weight = jax.random.normal(ks[1], (NUM_RELS, IN_FEAT, OUT_FEAT), dtype=jnp.float32) * 0.05
        loop_weight = jax.random.normal(ks[2], (IN_FEAT, OUT_FEAT), dtype=jnp.float32) * 0.05
        norm = jax.random.uniform(ks[3], (N_EDGES, 1), dtype=jnp.float32)
        src = jax.random.randint(ks[4], (N_EDGES,), 0, N_NODES, dtype=jnp.int32)
        dst = jax.random.randint(ks[5], (N_EDGES,), 0, N_NODES, dtype=jnp.int32)
        etypes = jax.random.randint(ks[6], (N_EDGES,), 0, NUM_RELS, dtype=jnp.int32)
        return {'feat': feat, 'weight': weight, 'loop_weight': loop_weight, 'norm': norm, 'src': src, 'dst': dst, 'etypes': etypes}
    _L3_gnn_all = _L3_gnn_setup()
    _L3_gnn_in = {k: v for k, v in _L3_gnn_all.items() if k in ('weight', 'loop_weight')}
    del _L3_gnn_all
    return {'x': x, 'src': src, 'dst': dst, 'edge_type_8': edge_type_8, 'edge_weight1': edge_weight1, 'L0_gnn_W': _L0_gnn_in['W'], 'L0_gnn_b': _L0_gnn_in['b'], 'L1_gnn_W1': _L1_gnn_in['W1'], 'L1_gnn_b1': _L1_gnn_in['b1'], 'L1_gnn_W2': _L1_gnn_in['W2'], 'L1_gnn_b2': _L1_gnn_in['b2'], 'L1_gnn_W4': _L1_gnn_in['W4'], 'L1_gnn_b4': _L1_gnn_in['b4'], 'L2_gnn_Wp': _L2_gnn_in['Wp'], 'L2_gnn_bp': _L2_gnn_in['bp'], 'L2_gnn_Wl': _L2_gnn_in['Wl'], 'L2_gnn_bl': _L2_gnn_in['bl'], 'L2_gnn_Wr': _L2_gnn_in['Wr'], 'L3_gnn_weight': _L3_gnn_in['weight'], 'L3_gnn_loop_weight': _L3_gnn_in['loop_weight']}

def reference(x, src, dst, edge_type_8, edge_weight1, L0_gnn_W, L0_gnn_b, L1_gnn_W1, L1_gnn_b1, L1_gnn_W2, L1_gnn_b2, L1_gnn_W4, L1_gnn_b4, L2_gnn_Wp, L2_gnn_bp, L2_gnn_Wl, L2_gnn_bl, L2_gnn_Wr, L3_gnn_weight, L3_gnn_loop_weight):
    import jax
    import jax.numpy as jnp

    def _L0_gnn_ref(x, edge_index, W, b):
        import jax, jax.numpy as jnp
        import numpy as np
        N_NODES = 3125
        IN_CH = 128
        OUT_CH = 128
        N_EDGES = 40000
        src, dst = (edge_index[0], edge_index[1])
        neighbor_sum = jax.ops.segment_sum(x[src], dst, num_segments=x.shape[0])
        neighbor_count = jax.ops.segment_sum(jnp.ones((src.shape[0],), dtype=x.dtype), dst, num_segments=x.shape[0])
        neighbor_mean = neighbor_sum / jnp.clip(neighbor_count, 1.0)[:, None]
        h = jnp.concatenate([x, neighbor_mean], axis=-1)
        return h @ W.T + b

    def _L1_gnn_ref(x, src, dst, W1, b1, W2, b2, W4, b4):
        import jax, jax.numpy as jnp
        import numpy as np
        N_NODES = 3125
        N_EDGES = 50000
        IN_FEAT = 128
        OUT_FEAT = 128
        n_nodes = x.shape[0]
        theta = x[dst] - x[src]
        w = jax.nn.sigmoid(jax.nn.relu(theta @ W1 + b1) @ W2 + b2)
        w_theta = w * theta
        agg = jax.ops.segment_sum(w_theta, dst, num_segments=n_nodes)
        indeg = jax.ops.segment_sum(jnp.ones((dst.shape[0], 1), x.dtype), dst, num_segments=n_nodes)
        return agg + indeg * (x @ W4 + b4)

    def _L2_gnn_ref(x, edge_index, Wp, bp, Wl, bl, Wr):
        import jax, jax.numpy as jnp
        import numpy as np
        N = 3125
        E = 50000
        D = 128
        EPS = 1e-12
        src, dst = (edge_index[0], edge_index[1])
        n = x.shape[0]
        h = jax.nn.relu(x @ Wp.T + bp)
        msg = h[src]
        agg = jax.ops.segment_sum(msg, dst, num_segments=n)
        cnt = jax.ops.segment_sum(jnp.ones((msg.shape[0],), x.dtype), dst, num_segments=n)
        mean = agg / jnp.maximum(cnt, 1.0)[:, None]
        out = mean @ Wl.T + bl + x @ Wr.T
        out = jax.nn.elu(out)
        norm = jnp.sqrt(jnp.sum(out * out, axis=-1, keepdims=True))
        out = out / jnp.maximum(norm, EPS)
        return x + out

    def _L3_gnn_ref(feat, weight, loop_weight, norm, src, dst, etypes):
        import jax, jax.numpy as jnp
        import numpy as np
        N_NODES = 625
        N_EDGES = 40000
        IN_FEAT = 128
        OUT_FEAT = 128
        NUM_RELS = 8
        all_h = jnp.einsum('ni,rio->rno', feat, weight)
        msg = all_h[etypes, src] * norm
        h = jax.ops.segment_sum(msg, dst, num_segments=feat.shape[0])
        h = h + feat @ loop_weight
        return h
    edge_index = jnp.stack([src, dst])
    h = jnp.maximum(_layernorm(x, axis=-1), 0.0)
    x = x + _L0_gnn_ref(h, edge_index, L0_gnn_W, L0_gnn_b)
    h = jnp.maximum(_layernorm(x, axis=-1), 0.0)
    x = x + _L1_gnn_ref(h, src, dst, L1_gnn_W1, L1_gnn_b1, L1_gnn_W2, L1_gnn_b2, L1_gnn_W4, L1_gnn_b4)
    h = jnp.maximum(_layernorm(x, axis=-1), 0.0)
    x = x + _L2_gnn_ref(h, edge_index, L2_gnn_Wp, L2_gnn_bp, L2_gnn_Wl, L2_gnn_bl, L2_gnn_Wr)
    h = jnp.maximum(_layernorm(x, axis=-1), 0.0)
    x = x + _L3_gnn_ref(h, L3_gnn_weight, L3_gnn_loop_weight, edge_weight1, src, dst, edge_type_8)
    return x

_drawn_inputs = setup_inputs


def setup_inputs(seed=0):
    import zlib

    import numpy as np

    out = dict(_drawn_inputs(seed))
    spreads = {}
    factors = {'L1_gnn_b1': 27.253,
     'L2_gnn_Wp': 64.0,
     'L2_gnn_bp': 64.0,
     'L2_gnn_Wl': 64.0,
     'L2_gnn_bl': 64.0,
     'L2_gnn_Wr': 64.0,
     'L3_gnn_loop_weight': 4.156}
    for name, (base, spread) in spreads.items():
        noise = np.random.default_rng([zlib.crc32(name.encode()), seed]).standard_normal(out[name].shape)
        drawn = base * np.exp(spread * noise) if base else spread * noise
        out[name] = jnp.asarray(drawn.astype(out[name].dtype))
    for name, factor in factors.items():
        out[name] = (out[name] * factor).astype(out[name].dtype)
    return out
```

```python
import concourse.bass as bass
from concourse import mybir
from concourse.alu_op_type import AluOpType as ALU
from contextlib import ExitStack

ACT = mybir.ActivationFunctionType
AXX = mybir.AxisListType.X
F32, I32, U32 = mybir.dt.float32, mybir.dt.int32, mybir.dt.uint32

P = 128
TPG = 4
WIN = 64
CH = 4
NSLOT = 7
NONE = 4
EPS_LN, EPS_NORM = 1e-5, 1e-12


class Sem:

    def __init__(self, handle):
        self.handle, self.value = handle, 0


class Queue:

    def __init__(self):
        self.items = []

    def do(self, make, sem=None, by=1):
        if sem is None:
            self.items.append(lambda eng: make(eng))
            return None
        sem.value += by
        self.items.append(lambda eng: make(eng).then_inc(sem.handle, by))
        return sem.value

    def dma(self, make, sem):
        return self.do(make, sem, 16)

    def wait(self, sem, value):
        if value:
            self.items.append(lambda eng: eng.wait_ge(sem.handle, value))

    def emit(self, eng):
        for item in self.items:
            item(eng)


def gnn_program(nc, ins, out):
    x_in = ins["x"]
    n_nodes, d = x_in.shape
    n_edges = ins["src"].shape[0]
    n_rel = ins["L3_gnn_weight"].shape[0]
    assert d == P
    nb = -(-n_nodes // P)
    npad = nb * P
    nt = -(-n_edges // P)
    ng = -(-nt // TPG)
    nr = -(-nt // P)
    chunks = [(c, min(CH, nb - c)) for c in range(0, nb, CH)]
    full_tiles = n_edges // P
    rest_edges = n_edges - full_tiles * P
    last_rows = n_nodes - (nb - 1) * P

    with ExitStack() as ctx:
        def sb(name, shape, dt=F32):
            return ctx.enter_context(nc.sbuf_tensor(name, shape, dt))

        def sem(name):
            return Sem(ctx.enter_context(nc.semaphore(name)))

        def dram(name, shape, dt=F32):
            return nc.dram_tensor(name, shape, dt, kind="Internal").ap()

        tab_h = dram("tab_h", (npad, P))
        tab_ph = dram("tab_ph", (npad, 2 * P))
        tab_pb = dram("tab_pb", (npad, P))
        tab_m = dram("tab_m", (npad, P))
        tab_rel = dram("tab_rel", (npad * n_rel, P))
        dst_flat = dram("dst_flat", (nr * P * P,))

        x = sb("x", [P, nb, P])
        h = sb("h", [P, nb, P])
        acc = sb("acc", [P, 2, npad])
        rself = acc[:, 1, :].rearrange("p (b f) -> p b f", f=P)
        rows = sb("rows", [P, NSLOT, TPG, 2 * P])
        spare = rows[:, :, :, :].rearrange("p a b c -> p (a b c)")
        stage = spare[:, 0:2 * CH * P].rearrange("p (s b f) -> p s b f", s=2, f=P)
        stage2 = spare[:, 2 * CH * P:4 * CH * P].rearrange("p (s b f) -> p s b f", s=2, f=P)
        stage_rel = spare[:, 0:3 * n_rel * P].rearrange("p (s f) -> p s f", s=3)
        raw = acc[:, :, :].rearrange("p k n -> p (k n)")
        idx_src = sb("idx_src", [P, nr * P], U32)
        idx_rel = sb("idx_rel", [P, nr * P], U32)
        dst_rel = sb("dst_rel", [P, nr * P])
        wt = sb("wt", [P, nr * P])
        win_node = sb("win_node", [P, ng])
        base_row = sb("base_row", [1, ng])
        base_int = sb("base_int", [1, ng], I32)
        oneh = sb("oneh", [P, NONE, TPG, WIN])
        onehT = sb("onehT", [WIN, 2, TPG * P])
        dst_bc = sb("dst_bc", [WIN, 3, TPG * P])
        pwin = sb("pwin", [WIN, 3, P])
        diff = sb("diff", [P, 2, TPG, P])
        zed = sb("zed", [P, 2, TPG])
        gate = sb("gate", [P, 2, TPG])
        hT = sb("hT", [P, 2, CH * P])
        stats = sb("stats", [P, nb, 6])
        mv = sb("mv", [P, nb, 2])
        std = sb("std", [P, nb])
        rstd = sb("rstd", [P, nb])
        indeg = sb("indeg", [P, nb])
        rdeg = sb("rdeg", [P, nb])
        sumw = sb("sumw", [P, nb])
        tmp = sb("tmp", [P, 2, CH, P])
        tmp2 = sb("tmp2", [P, 2, CH, P])
        nrm = sb("nrm", [P, nb])
        ident = sb("ident", [P, P])
        ones = sb("ones", [P, P])
        iota_b = sb("iota_b", [P, P])
        iota_w = iota_b[:, 0:WIN]
        iota_p = sb("iota_p", [P, 1])
        eps_ln = sb("eps_ln", [P, 1])
        b2 = sb("b2", [P, 1])
        w0 = sb("w0", [P, 2 * P])
        w0a, w0b = sb("w0a", [P, P]), sb("w0b", [P, P])
        w1, w4 = sb("w1", [P, P]), sb("w4", [P, P])
        wp, wl, wr = sb("wp", [P, P]), sb("wl", [P, P]), sb("wr", [P, P])
        wpT, wlT, wrT = sb("wpT", [P, P]), sb("wlT", [P, P]), sb("wrT", [P, P])
        wrel = sb("wrel", [P, n_rel * P])
        wloop = sb("wloop", [P, P])
        bias0, bias1, bias4, biasp, biasl, w2 = (sb(n, [P, P]) for n in ("bias0", "bias1", "bias4", "biasp", "biasl", "w2"))
        n_inside = sb("n_inside", [P, 1])
        outside = sb("outside", [1, 1], I32)
        gen_idx = sb("gen_idx", [P, TPG], U32)
        gen_tgt = sb("gen_tgt", [P, TPG], U32)
        gen_dst = sb("gen_dst", [P, TPG])
        gen_abs = sb("gen_abs", [P, TPG])
        gen_in = sb("gen_in", [P, TPG])
        gen_wt = sb("gen_wt", [P, TPG])

        ps = [ctx.enter_context(nc.psum_tensor(f"ps{i}", [P, 512], F32)) for i in range(8)]
        ps_t, ps_m, ps_e, ps_a = ps[0:2], ps[2:4], ps[4:6], ps[6:8]

        s_const = sem("s_const")
        s_win = sem("s_win")
        s_wgt = sem("s_wgt")
        s_xin = sem("s_xin")
        s_pad = sem("s_pad")
        s_prep = sem("s_prep")
        s_prepT = sem("s_prepT")
        s_dstf = sem("s_dstf")
        s_ln = sem("s_ln")
        s_sqrt = sem("s_sqrt")
        s_h = sem("s_h")
        s_tr = sem("s_tr")
        s_hT = sem("s_hT")
        s_mm = sem("s_mm")
        s_node = sem("s_node")
        s_relu = sem("s_relu")
        s_tab = [sem(f"s_tab{i}") for i in range(3)]
        s_tab2 = [sem(f"s_tab2{i}") for i in range(2)]
        s_tabh = sem("s_tabh")
        s_zero = sem("s_zero")
        s_row = [sem(f"s_row{i}") for i in range(NSLOT)]
        s_one = sem("s_one")
        s_scat = sem("s_scat")
        s_add = sem("s_add")
        s_bc = [sem(f"s_bc{i}") for i in range(3)]
        s_pw = [sem(f"s_pw{i}") for i in range(3)]
        s_oneT = sem("s_oneT")
        s_exp = sem("s_exp")
        s_dif = sem("s_dif")
        s_gate = sem("s_gate")
        s_cnt = sem("s_cnt")
        s_out = sem("s_out")
        s_gen = sem("s_gen")
        gen_sems = [{k: ctx.enter_context(nc.semaphore(f"g{layer}_{k}")) for k in
                     ("idx", "row", "prow", "z", "gate", "one", "scat", "seen")} for layer in range(4)]

        pe, dve, act, pool, sp = (Queue() for _ in range(5))

        pool.do(lambda e: e.memset(ident[:, :], 0.0), s_const)
        pool.do(lambda e: e.memset(ones[:, :], 1.0), s_const)
        pool.do(lambda e: e.memset(eps_ln[:, :], EPS_LN), s_const)
        pool.do(lambda e: e.iota(iota_b[:, :], [[1, P]], base=0, channel_multiplier=0,
                                 allow_small_or_imprecise_dtypes=True), s_const)
        n = pool.do(lambda e: e.iota(iota_p[:, :], [[1, 1]], base=0, channel_multiplier=1,
                                     allow_small_or_imprecise_dtypes=True), s_const)
        pool.wait(s_const, n)
        n_const = pool.do(lambda e: e.affine_select(
            out=ident[:, :], in_=ident[:, :], compare_op=ALU.not_equal, fill=1.0,
            base=0, pattern=[[-1, P]], channel_multiplier=1), s_const)

        rblk = nr * P
        raw_src = raw[:, 0 * rblk:1 * rblk].bitcast(I32)
        raw_dst = raw[:, 1 * rblk:2 * rblk].bitcast(I32)
        raw_typ = raw[:, 2 * rblk:3 * rblk].bitcast(I32)
        raw_wt = raw[:, 3 * rblk:4 * rblk]
        flt = h[:, :, :].rearrange("p b f -> p (b f)")
        f_src, f_dst, f_rel = (flt[:, i * rblk:(i + 1) * rblk] for i in range(3))
        assert 4 * rblk <= 2 * npad and 3 * rblk <= npad
        body = (nr - 1) * P
        tail = full_tiles - body
        pads = ((raw_src, 0), (raw_dst, -1), (raw_typ, 0), (raw_wt, 0))
        for v, fill in pads:
            n_pad = dve.do(lambda e, v=v, fill=fill: e.memset(v[:, body:rblk], fill), s_pad)
        sp.wait(s_pad, n_pad)
        for name, v in (("src", raw_src), ("dst", raw_dst), ("edge_type_8", raw_typ), ("edge_weight1", raw_wt)):
            a = ins[name]
            if len(a.shape) == 2:
                a = a.rearrange("n o -> (n o)")
            v3 = v.rearrange("p (b e) -> p b e", e=P)
            sp.dma(lambda e, a=a, v3=v3: e.dma_start(
                v3[:, 0:nr - 1, :], a[0:body * P].rearrange("(b p e) -> p b e", p=P, e=P)), s_win)
            sp.dma(lambda e, a=a, v3=v3: e.dma_start(
                v3[0:tail, nr - 1, :], a[body * P:full_tiles * P].rearrange("(p e) -> p e", e=P)), s_win)
            if rest_edges:
                n_win = sp.dma(lambda e, a=a, v3=v3: e.dma_start(
                    v3[tail:tail + 1, nr - 1, 0:rest_edges],
                    a[full_tiles * P:n_edges].rearrange("(p e) -> p e", p=1)), s_win)
        n_win = s_win.value
        dve.do(lambda e: e.memset(x[:, nb - 1, :], 0.0), s_pad)
        sp.wait(s_pad, s_pad.value)
        sp.dma(lambda e: e.dma_start(x[:, 0:nb - 1, :],
                                     x_in[0:(nb - 1) * P, :].rearrange("(b p) f -> p b f", p=P)), s_xin)
        n_xin = sp.dma(lambda e: e.dma_start(x[0:last_rows, nb - 1, :], x_in[(nb - 1) * P:n_nodes, :]), s_xin)

        for t, a in ((w0, ins["L0_gnn_W"]), (w1, ins["L1_gnn_W1"]), (w4, ins["L1_gnn_W4"]), (wp, ins["L2_gnn_Wp"]),
                     (wl, ins["L2_gnn_Wl"]), (wr, ins["L2_gnn_Wr"]), (wloop, ins["L3_gnn_loop_weight"])):
            act.dma(lambda e, t=t, a=a: e.dma_start(t[:, :], a), s_wgt)
        act.dma(lambda e: e.dma_start(wrel[:, :].rearrange("p (r o) -> p r o", r=n_rel),
                                      ins["L3_gnn_weight"].rearrange("r i o -> i r o")), s_wgt)
        for t, a in ((bias0, ins["L0_gnn_b"]), (bias1, ins["L1_gnn_b1"]), (bias4, ins["L1_gnn_b4"]),
                     (biasp, ins["L2_gnn_bp"]), (biasl, ins["L2_gnn_bl"]),
                     (w2, ins["L1_gnn_W2"].rearrange("n o -> (n o)")), (b2, ins["L1_gnn_b2"])):
            act.dma(lambda e, t=t, a=a: e.dma_start(t[:, :], a.partition_broadcast(P)), s_wgt)
        n_wgt = s_wgt.value

        dve.wait(s_win, n_win)
        dve.do(lambda e: e.tensor_copy(f_src, raw_src), s_prep)
        n_dst = dve.do(lambda e: e.tensor_copy(f_dst, raw_dst), s_prep)
        n = dve.do(lambda e: e.tensor_copy(f_rel, raw_typ), s_prep)
        dve.wait(s_prep, n)
        n_flt = dve.do(lambda e: e.scalar_tensor_tensor(out=f_rel, in0=f_src, scalar=float(n_rel), in1=f_rel,
                                                op0=ALU.mult, op1=ALU.add), s_prep)
        sp.wait(s_prep, n_dst)
        n_dstf = sp.dma(lambda e: e.dma_start(dst_flat.rearrange("(b p e) -> p b e", p=P, e=P),
                                     f_dst.rearrange("p (b e) -> p b e", e=P)), s_dstf)

        pe.wait(s_const, n_const)
        pe.wait(s_prep, n_flt)
        bank_free = {}
        k = 0
        for srcv, dstv in ((f_dst, dst_rel), (f_src, idx_src), (f_rel, idx_rel), (raw_wt, wt)):
            for b0 in range(0, nr, CH):
                m = min(CH, nr - b0)
                bank = ps_t[k % 2]
                pe.wait(s_prep, bank_free.get(k % 2, 0))
                for j in range(m):
                    blk = srcv[:, (b0 + j) * P:(b0 + j + 1) * P]
                    ins_ = (lambda e, bank=bank, j=j, blk=blk: e.transpose(bank[:, j * P:(j + 1) * P], blk, ident[:, :]))
                    n = pe.do(ins_, s_prepT) if j == m - 1 else pe.do(ins_)
                dve.wait(s_prepT, n)
                bank_free[k % 2] = dve.do(lambda e, bank=bank, b0=b0, m=m, dstv=dstv: e.tensor_copy(
                    dstv[:, b0 * P:(b0 + m) * P], bank[:, 0:m * P]), s_prep)
                k += 1
        n_tab = s_prep.value
        dve.wait(s_prep, n_tab)
        first = dst_rel[0:1, 0:ng * TPG].rearrange("p (g t) -> p g t", t=TPG)[:, :, 0]
        dve.do(lambda e: e.tensor_scalar(base_row[:, :], first, float(npad - WIN), None, ALU.min), s_prep)
        dve.wait(s_prep, s_prep.value)
        n_base = dve.do(lambda e: e.tensor_copy(base_int[:, :], base_row[:, :]), s_prep)
        pe.wait(s_prep, n_base)
        n = pe.do(lambda e: e.matmul(ps_t[0][:, 0:ng], ones[0:1, :], base_row[:, :], start=True, stop=True), s_prepT)
        dve.wait(s_prepT, n)
        gd = dst_rel[:, 0:ng * TPG].rearrange("p (g t) -> p g t", t=TPG)
        n = dve.do(lambda e: e.tensor_tensor(out=gd, in0=gd, in1=ps_t[0][:, 0:ng].unsqueeze(2).to_broadcast([P, ng, TPG]),
                                         op=ALU.subtract), s_prep)
        n_prep = dve.do(lambda e: e.tensor_scalar(win_node[:, :], ps_t[0][:, 0:ng], iota_p[:, 0:1], None, ALU.add), s_prep)

        gi = f_rel[:, 0:ng * TPG].rearrange("p (g t) -> p g t", t=TPG)
        dve.wait(s_prep, n_prep)
        n = dve.do(lambda e: e.tensor_scalar(gi, gd, 0.0, None, ALU.is_ge), s_prep)
        dve.wait(s_prep, n)
        n = dve.do(lambda e: e.scalar_tensor_tensor(out=gi, in0=gd, scalar=float(WIN), in1=gi, op0=ALU.is_lt, op1=ALU.mult), s_prep)
        dve.wait(s_prep, n)
        n = dve.do(lambda e: e.tensor_reduce(out=n_inside[:, :], in_=f_rel[:, 0:ng * TPG], axis=AXX, op=ALU.add), s_prep)
        pe.wait(s_prep, n)
        n = pe.do(lambda e: e.matmul(ps_t[0][:, 0:1], ones[:, :], n_inside[:, :], start=True, stop=True), s_prepT)
        dve.wait(s_prepT, n)
        dve.do(lambda e: e.tensor_scalar(outside[:, :], ps_t[0][0:1, 0:1], -1.0, float(n_edges), ALU.mult, ALU.add), s_prep)

        pe.wait(s_wgt, n_wgt)
        for srcv, dstv in ((w0[:, 0:P], w0a), (w0[:, P:2 * P], w0b), (wp[:, :], wpT), (wl[:, :], wlT), (wr[:, :], wrT)):
            pe.wait(s_prep, s_prep.value)
            n = pe.do(lambda e, srcv=srcv: e.transpose(ps_t[1][:, 0:P], srcv, ident[:, :]), s_prepT)
            dve.wait(s_prepT, n)
            dve.do(lambda e, dstv=dstv: e.tensor_copy(dstv[:, :], ps_t[1][:, 0:P]), s_prep)
        n_prep = s_prep.value
        dve.wait(s_prep, n_prep)
        dve.wait(s_wgt, n_wgt)
        dve.wait(s_xin, n_xin)
        dve.wait(s_const, n_const)
        for q in (pe, act, pool, sp):
            q.wait(s_prep, n_prep)
        act.wait(s_wgt, n_wgt)
        act.wait(s_const, n_const)
        for q in (sp, dve, act):
            q.wait(s_dstf, n_dstf)
        n_zero = pool.do(lambda e: e.memset(acc[:, :, :], 0.0), s_zero)

        st = {"bank": 0}
        node_free = {}
        x_ready = {}

        def wait_free(q, key):
            for s, v in node_free.get(key, ()):
                q.wait(s, v)

        def layernorm(c, m):
            dve.wait(s_node, x_ready.get(c, 0))
            for b in range(c, c + m):
                n = dve.do(lambda e, b=b: e.bn_stats(stats[:, b, :], x[:, b, :]), s_ln)
            dve.wait(s_ln, n)
            for b in range(c, c + m):
                n = dve.do(lambda e, b=b: e.bn_aggr(mv[:, b, :], stats[:, b, :]), s_ln)
            act.wait(s_ln, n)
            n2 = act.do(lambda e: e.activation(std[:, c:c + m], mv[:, c:c + m, 1], ACT.Sqrt, bias=eps_ln[:, 0:1]), s_sqrt)
            dve.wait(s_ln, n)
            wait_free(dve, "h%d" % c)
            for b in range(c, c + m):
                n3 = dve.do(lambda e, b=b: e.tensor_scalar(h[:, b, :], x[:, b, :], mv[:, b, 0:1], None, ALU.subtract), s_ln)
            dve.wait(s_sqrt, n2)
            n4 = dve.do(lambda e: e.reciprocal(rstd[:, c:c + m], std[:, c:c + m]), s_ln)
            act.wait(s_ln, n4)
            for b in range(c, c + m):
                n = act.do(lambda e, b=b: e.activation(h[:, b, :], h[:, b, :], ACT.Relu, scale=rstd[:, b:b + 1]), s_h)
            return n

        def transposed(blocks, ready, slot):
            bank = ps_t[slot]
            for s, v in ready:
                pe.wait(s, v)
            wait_free(pe, "ps_t%d" % slot)
            for j, blk in enumerate(blocks):
                f = lambda e, j=j, blk=blk: e.transpose(bank[:, j * P:(j + 1) * P], blk, ident[:, :])
                n = pe.do(f, s_tr) if j == len(blocks) - 1 else pe.do(f)
            act.wait(s_tr, n)
            wait_free(act, "hT%d" % slot)
            m = len(blocks)
            n = act.do(lambda e: e.copy(hT[:, slot, 0:m * P], bank[:, 0:m * P]), s_hT)
            node_free["ps_t%d" % slot] = [(s_hT, n)]
            return n

        def product(slot, m, weight, ready):
            k = st["bank"] % 2
            st["bank"] += 1
            bank, key = ps_m[k], "ps_m%d" % k
            for s, v in ready:
                pe.wait(s, v)
            wait_free(pe, key)
            for j in range(m):
                f = lambda e, j=j: e.matmul(bank[:, j * P:(j + 1) * P], hT[:, slot, j * P:(j + 1) * P], weight[:, :],
                                            start=True, stop=True)
                n = pe.do(f, s_mm) if j == m - 1 else pe.do(f)
            return bank[:, 0:m * P].rearrange("p (b f) -> p b f", f=P), n, key

        def bcast(v, m):
            return v[:, :].unsqueeze(1).to_broadcast([P, m, P])

        def xadd(c, m, make):
            dve.wait(s_node, x_ready.get(c, 0))
            x_ready[c] = dve.do(make, s_node)
            return x_ready[c]

        tab_done = {}

        def table_write(make, s):
            n = sp.dma(make, s)
            tab_done[s] = n
            return n

        def rows_of(tab, c, m):
            return tab[c * P:(c + m) * P, :].rearrange("(b p) f -> p b f", p=P)

        def self_term(layer, c, m, slot, n_h, n_hT):
            xc = x[:, c:c + m, :]
            if layer == 0:
                v, n, key = product(slot, m, w0a, [(s_hT, n_hT)])
                node_free["hT%d" % slot] = [(s_mm, n)]
                dve.wait(s_mm, n)
                n = xadd(c, m, lambda e: e.tensor_tensor(out=xc, in0=v, in1=xc, op=ALU.add))
                node_free[key] = [(s_node, n)]
                xadd(c, m, lambda e: e.tensor_tensor(out=xc, in0=xc, in1=bcast(bias0, m), op=ALU.add))
            elif layer == 1:
                v, n, key = product(slot, m, w4, [(s_hT, n_hT)])
                node_free["hT%d" % slot] = [(s_mm, n)]
                dve.wait(s_mm, n)
                wait_free(dve, "tmp%d" % slot)
                n = dve.do(lambda e: e.tensor_tensor(out=tmp[:, slot, 0:m, :], in0=v, in1=bcast(bias4, m), op=ALU.add), s_node)
                node_free[key] = [(s_node, n)]
                dve.wait(s_node, n)
                dve.wait(s_node, x_ready.get(c, 0))
                for j in range(m):
                    n = dve.do(lambda e, j=j: e.scalar_tensor_tensor(
                        out=x[:, c + j, :], in0=tmp[:, slot, j, :], scalar=indeg[:, c + j:c + j + 1],
                        in1=x[:, c + j, :], op0=ALU.mult, op1=ALU.add), s_node)
                x_ready[c] = n
                node_free["tmp%d" % slot] = [(s_node, n)]
            elif layer == 2:
                v, n, key = product(slot, m, wrT, [(s_hT, n_hT)])
                node_free["hT%d" % slot] = [(s_mm, n)]
                dve.wait(s_mm, n)
                wait_free(dve, "sums_read")
                n = dve.do(lambda e: e.tensor_tensor(out=rself[:, c:c + m, :], in0=v, in1=bcast(biasl, m), op=ALU.add), s_node)
                node_free[key] = [(s_node, n)]
                dve.wait(s_h, n_h)
                n = xadd(c, m, lambda e: e.tensor_tensor(out=xc, in0=xc, in1=h[:, c:c + m, :], op=ALU.add))
                node_free["h%d" % c] = [(s_node, n)]
            else:
                v, n, key = product(slot, m, wloop, [(s_hT, n_hT)])
                node_free["hT%d" % slot] = [(s_mm, n)]
                dve.wait(s_mm, n)
                n = xadd(c, m, lambda e: e.tensor_tensor(out=xc, in0=v, in1=xc, op=ALU.add))
                node_free[key] = [(s_node, n)]

        def node_pre(layer, i, c, m):
            n_h = layernorm(c, m)
            slot = i % 2
            hc = h[:, c:c + m, :]
            blocks = [h[:, b, :] for b in range(c, c + m)]
            n_hT = transposed(blocks, [(s_h, n_h)], slot)
            node_free["h%d" % c] = [(s_tr, s_tr.value)]
            pe_ready = [(s_hT, n_hT)]
            if layer == 0:
                sp.wait(s_h, n_h)
                table_write(lambda e: e.dma_start(rows_of(tab_h, c, m), hc), s_tabh)
            elif layer == 1:
                sp.wait(s_h, n_h)
                table_write(lambda e: e.dma_start(rows_of(tab_ph, c, m)[:, :, P:2 * P], hc), s_tabh)
                v, n, key = product(slot, m, w1, pe_ready)
                act.wait(s_mm, n)
                wait_free(act, "stage%d" % slot)
                na = act.do(lambda e: e.copy(stage[:, slot, 0:m, :], v), s_relu)
                dve.wait(s_relu, na)
                wait_free(dve, "stage2%d" % slot)
                nd = dve.do(lambda e: e.tensor_tensor(out=stage2[:, slot, 0:m, :], in0=v, in1=bcast(bias1, m), op=ALU.add), s_node)
                node_free[key] = [(s_relu, na), (s_node, nd)]
                sp.wait(s_relu, na)
                nt_ = table_write(lambda e: e.dma_start(rows_of(tab_ph, c, m)[:, :, 0:P], stage[:, slot, 0:m, :]), s_tab[slot])
                node_free["stage%d" % slot] = [(s_tab[slot], nt_)]
                sp.wait(s_node, nd)
                nt_ = table_write(lambda e: e.dma_start(rows_of(tab_pb, c, m), stage2[:, slot, 0:m, :]), s_tab2[slot])
                node_free["stage2%d" % slot] = [(s_tab2[slot], nt_)]
            elif layer == 2:
                v, n, key = product(slot, m, wpT, pe_ready)
                dve.wait(s_mm, n)
                wait_free(dve, "stage2%d" % slot)
                nd = dve.do(lambda e: e.tensor_tensor(out=stage2[:, slot, 0:m, :], in0=v, in1=bcast(biasp, m), op=ALU.add), s_node)
                node_free[key] = [(s_node, nd)]
                act.wait(s_node, nd)
                wait_free(act, "stage%d" % slot)
                na = act.do(lambda e: e.activation(stage[:, slot, 0:m, :], stage2[:, slot, 0:m, :], ACT.Relu), s_relu)
                node_free["stage2%d" % slot] = [(s_relu, na)]
                sp.wait(s_relu, na)
                nt_ = table_write(lambda e: e.dma_start(rows_of(tab_m, c, m), stage[:, slot, 0:m, :]), s_tab[slot])
                node_free["stage%d" % slot] = [(s_tab[slot], nt_)]
            else:
                half = n_rel * P // 2
                rel_rows = tab_rel.rearrange("(n r) f -> n (r f)", r=n_rel)
                for j in range(m):
                    b = c + j
                    sl = b % 3
                    wait_free(act, "rel%d" % sl)
                    wait_free(dve, "rel%d" % sl)
                    for part in range(2):
                        k = st["bank"] % 2
                        st["bank"] += 1
                        bank, key = ps_m[k], "ps_m%d" % k
                        pe.wait(s_hT, n_hT)
                        wait_free(pe, key)
                        n = pe.do(lambda e, j=j, part=part, bank=bank: e.matmul(
                            bank[:, 0:half], hT[:, slot, j * P:(j + 1) * P], wrel[:, part * half:(part + 1) * half],
                            start=True, stop=True), s_mm)
                        dstv = stage_rel[:, sl, part * half:(part + 1) * half]
                        if part == 0:
                            act.wait(s_mm, n)
                            na = act.do(lambda e, bank=bank, dstv=dstv: e.copy(dstv, bank[:, 0:half]), s_relu)
                            node_free[key] = [(s_relu, na)]
                        else:
                            dve.wait(s_mm, n)
                            nd = dve.do(lambda e, bank=bank, dstv=dstv: e.tensor_copy(dstv, bank[:, 0:half]), s_node)
                            node_free[key] = [(s_node, nd)]
                    sp.wait(s_relu, na)
                    sp.wait(s_node, nd)
                    nt_ = table_write(lambda e, b=b, sl=sl: e.dma_start(rel_rows[b * P:(b + 1) * P, :], stage_rel[:, sl, :]), s_tab[sl])
                    node_free["rel%d" % sl] = [(s_tab[sl], nt_)]
            self_term(layer, c, m, slot, n_h, n_hT)

        def node_post(layer, i, c, m, ready):
            xc = x[:, c:c + m, :]
            cols = [acc[:, 0, b * P:(b + 1) * P] for b in range(c, c + m)]
            k = st["bank"] % 2
            st["bank"] += 1
            bank, key = ps_m[k], "ps_m%d" % k
            for s, v in ready:
                pe.wait(s, v)
            wait_free(pe, key)
            weight = {0: w0b, 2: wlT}.get(layer)
            for j in range(m):
                if weight is None:
                    f = lambda e, j=j: e.transpose(bank[:, j * P:(j + 1) * P], cols[j], ident[:, :])
                else:
                    f = lambda e, j=j: e.matmul(bank[:, j * P:(j + 1) * P], cols[j], weight[:, :], start=True, stop=True)
                n = pe.do(f, s_mm) if j == m - 1 else pe.do(f)
            v = bank[:, 0:m * P].rearrange("p (b f) -> p b f", f=P)
            acc_read.append(n)
            slot = i % 2
            dve.wait(s_mm, n)
            if layer == 0:
                dve.wait(s_node, x_ready[c])
                for j in range(m):
                    n = dve.do(lambda e, j=j: e.scalar_tensor_tensor(
                        out=x[:, c + j, :], in0=v[:, j, :], scalar=rdeg[:, c + j:c + j + 1], in1=x[:, c + j, :],
                        op0=ALU.mult, op1=ALU.add), s_node)
                x_ready[c] = n
                node_free[key] = [(s_node, n)]
            elif layer == 1:
                dve.wait(s_node, x_ready[c])
                for j in range(m):
                    n = dve.do(lambda e, j=j: e.scalar_tensor_tensor(
                        out=x[:, c + j, :], in0=h[:, c + j, :], scalar=sumw[:, c + j:c + j + 1], in1=x[:, c + j, :],
                        op0=ALU.mult, op1=ALU.add), s_node)
                x_ready[c] = n
                n = xadd(c, m, lambda e: e.tensor_tensor(out=xc, in0=xc, in1=v, op=ALU.subtract))
                node_free[key] = [(s_node, n)]
                node_free["h%d" % c] = node_free["h%d" % c] + [(s_node, n)]
            elif layer == 2:
                o, o2 = tmp[:, slot, 0:m, :], tmp2[:, slot, 0:m, :]
                wait_free(dve, "tmp%d" % slot)
                for j in range(m):
                    n = dve.do(lambda e, j=j: e.scalar_tensor_tensor(
                        out=o[:, j, :], in0=v[:, j, :], scalar=rdeg[:, c + j:c + j + 1], in1=rself[:, c + j, :],
                        op0=ALU.mult, op1=ALU.add), s_node)
                node_free[key] = [(s_node, n)]
                dve.wait(s_node, n)
                n = dve.do(lambda e: e.tensor_scalar(o2, o, 0.0, None, ALU.min), s_node)
                act.wait(s_node, n)
                na = act.do(lambda e: e.activation(o2, o2, ACT.Exp), s_relu)
                n = dve.do(lambda e: e.tensor_scalar(o, o, 0.0, None, ALU.max), s_node)
                dve.wait(s_node, n)
                dve.wait(s_relu, na)
                n = dve.do(lambda e: e.scalar_tensor_tensor(out=o, in0=o2, scalar=-1.0, in1=o, op0=ALU.add, op1=ALU.add), s_node)
                dve.wait(s_node, n)
                n = dve.do(lambda e: e.tensor_tensor(out=o2, in0=o, in1=o, op=ALU.mult), s_node)
                dve.wait(s_node, n)
                n = dve.do(lambda e: e.tensor_reduce(out=nrm[:, c:c + m], in_=o2, axis=AXX, op=ALU.add), s_node)
                act.wait(s_node, n)
                na = act.do(lambda e: e.activation(nrm[:, c:c + m], nrm[:, c:c + m], ACT.Sqrt), s_relu)
                dve.wait(s_relu, na)
                n = dve.do(lambda e: e.tensor_scalar(nrm[:, c:c + m], nrm[:, c:c + m], EPS_NORM, None, ALU.max), s_node)
                dve.wait(s_node, n)
                n = dve.do(lambda e: e.reciprocal(nrm[:, c:c + m], nrm[:, c:c + m]), s_node)
                dve.wait(s_node, n)
                dve.wait(s_node, x_ready[c])
                for j in range(m):
                    n = dve.do(lambda e, j=j: e.scalar_tensor_tensor(
                        out=x[:, c + j, :], in0=o[:, j, :], scalar=nrm[:, c + j:c + j + 1], in1=x[:, c + j, :],
                        op0=ALU.mult, op1=ALU.add), s_node)
                x_ready[c] = n
                node_free["tmp%d" % slot] = [(s_node, n)]
            else:
                n = xadd(c, m, lambda e: e.tensor_tensor(out=xc, in0=v, in1=xc, op=ALU.add))
                node_free[key] = [(s_node, n)]
                sp.wait(s_node, n)
                last = c + m == nb
                full = m - 1 if last else m
                if full:
                    sp.dma(lambda e: e.dma_start(out[c * P:(c + full) * P, :].rearrange("(b p) f -> p b f", p=P),
                                                 x[:, c:c + full, :]), s_out)
                if last:
                    sp.dma(lambda e: e.dma_start(out[(nb - 1) * P:n_nodes, :], x[0:last_rows, nb - 1, :]), s_out)

        gcount = {"n": 0}
        slot_free = {}

        def edges(layer, n_zero):
            table, idx, width = {0: (tab_h, idx_src, P), 1: (tab_ph, idx_src, 2 * P),
                                 2: (tab_m, idx_src, P), 3: (tab_rel, idx_rel, P)}[layer]
            feat = slice(P, 2 * P) if layer == 1 else slice(0, P)
            for s, v in tab_done.items():
                pool.wait(s, v)
                if layer == 1:
                    sp.wait(s, v)
            tab_done.clear()
            tiles = [min(TPG, nt - g * TPG) for g in range(ng)]
            one_free, bc_free, oneT_free, exp_free, dif_free, gate_free, a_free = {}, {}, {}, {}, {}, {}, {}
            n_row, n_one, n_scat, n_bc, n_pw, n_oneT, n_exp, n_z, n_gate, n_sub = ({} for _ in range(10))
            sums = 2 if layer < 2 else 1

            def gather(g):
                sl = g % NSLOT
                for s, v in slot_free.get(sl, ()):
                    pool.wait(s, v)
                for t in range(tiles[g]):
                    col = g * TPG + t
                    n_row[g] = pool.dma(lambda e, t=t, col=col: e.indirect_dma_start(
                        out=rows[:, sl, t, 0:width], out_offset=None, in_=table[:, :],
                        in_offset=bass.IndirectOffsetOnAxis(ap=idx[:, col:col + 1], axis=0)), s_row[sl])

            def onehot(g):
                sl, m = g % NONE, tiles[g]
                o = oneh[:, sl, 0:m, :]
                rel = dst_rel[:, g * TPG:g * TPG + m].unsqueeze(2).to_broadcast([P, m, WIN])
                if g >= NONE:
                    dve.wait(s_scat, n_scat[g - NONE])
                n = dve.do(lambda e: e.tensor_tensor(out=o, in0=iota_w.unsqueeze(1).to_broadcast([P, m, WIN]),
                                                     in1=rel, op=ALU.is_equal), s_one)
                if layer == 3:
                    dve.wait(s_one, n)
                    n = dve.do(lambda e: e.tensor_tensor(
                        out=o, in0=o, in1=wt[:, g * TPG:g * TPG + m].unsqueeze(2).to_broadcast([P, m, WIN]), op=ALU.mult), s_one)
                n_one[g] = n

            def scatter(g):
                sl, m = g % NONE, tiles[g]
                bank = ps_a[g % 2]
                pe.wait(s_one, n_one[g])
                pe.wait(s_row[g % NSLOT], n_row[g])
                pe.wait(s_add, a_free.get(g % 2, 0))
                for t in range(m):
                    f = lambda e, t=t: e.matmul(bank[:, 0:WIN], rows[:, g % NSLOT, t, feat], oneh[:, sl, t, :],
                                                start=t == 0, stop=t == m - 1)
                    last = sums == 1 and t == m - 1
                    n = pe.do(f, s_scat) if last else pe.do(f)
                if sums == 2:
                    for t in range(m):
                        f = lambda e, t=t: e.matmul(bank[:, WIN:2 * WIN], ones[:, :], oneh[:, sl, t, :],
                                                    start=t == 0, stop=t == m - 1)
                        n = pe.do(f, s_scat) if t == m - 1 else pe.do(f)
                n_scat[g] = n
                slot_free[g % NSLOT] = [(s_scat, n)]

            def accumulate(g):
                dve.wait(s_scat, n_scat[g])
                if s_add.value:
                    dve.wait(s_add, s_add.value)

                def make(e):
                    start = e.value_load(base_int[0:1, g:g + 1], min_val=0, max_val=npad - WIN)
                    a = acc[:, 0:sums, bass.ds(start, WIN)]
                    v = ps_a[g % 2][:, 0:sums * WIN].rearrange("p (k w) -> p k w", k=sums)
                    return e.tensor_tensor(out=a, in0=a, in1=v, op=ALU.add)
                a_free[g % 2] = dve.do(make, s_add)

            def fetch_window(g):
                sl, m = g % 3, tiles[g]
                if g >= 3:
                    sp.wait(s_oneT, n_oneT[g - 3])
                    sp.wait(s_exp, n_exp[g - 3])
                n_bc[g] = sp.dma(lambda e: e.dma_start(
                    dst_bc[:, sl, 0:m * P], dst_flat[g * TPG * P:(g * TPG + m) * P].partition_broadcast(WIN)), s_bc[sl])

                def make(e):
                    start = e.value_load(base_int[0:1, g:g + 1], min_val=0, max_val=npad - WIN)
                    return e.dma_start(pwin[:, sl, :], tab_pb[bass.ds(start, WIN), :])
                n_pw[g] = sp.dma(make, s_pw[sl])

            def onehot_t(g):
                m = tiles[g]
                dve.wait(s_bc[g % 3], n_bc[g])
                if g >= 2:
                    dve.wait(s_exp, n_exp[g - 2])
                n_oneT[g] = dve.do(lambda e: e.tensor_scalar(
                    onehT[:, g % 2, 0:m * P], dst_bc[:, g % 3, 0:m * P], win_node[0:WIN, g:g + 1], None, ALU.is_equal), s_oneT)

            def spread(g):
                m = tiles[g]
                pe.wait(s_oneT, n_oneT[g])
                pe.wait(s_pw[g % 3], n_pw[g])
                if g >= 2:
                    pe.wait(s_dif, n_sub[g - 2])
                for t in range(m):
                    f = lambda e, t=t: e.matmul(ps_e[g % 2][:, t * P:(t + 1) * P], onehT[:, g % 2, t * P:(t + 1) * P],
                                                pwin[:, g % 3, :], start=True, stop=True)
                    n = pe.do(f, s_exp) if t == m - 1 else pe.do(f)
                n_exp[g] = n

            def logits(g):
                m, sl = tiles[g], g % 2
                dd = diff[:, sl, 0:m, :]
                dve.wait(s_exp, n_exp[g])
                dve.wait(s_row[g % NSLOT], n_row[g])
                n = dve.do(lambda e: e.tensor_tensor(
                    out=dd, in0=ps_e[sl][:, 0:m * P].rearrange("p (t f) -> p t f", f=P),
                    in1=rows[:, g % NSLOT, 0:m, 0:P], op=ALU.subtract), s_dif)
                n_sub[g] = n
                dve.wait(s_dif, n)
                n = dve.do(lambda e: e.scalar_tensor_tensor(out=dd, in0=dd, scalar=0.0, in1=bcast(w2, m),
                                                            op0=ALU.max, op1=ALU.mult), s_dif)
                dve.wait(s_dif, n)
                if g >= 2:
                    dve.wait(s_gate, n_gate[g - 2])
                n_z[g] = dve.do(lambda e: e.tensor_reduce(out=zed[:, sl, 0:m], in_=dd, axis=AXX, op=ALU.add), s_dif)
                act.wait(s_dif, n_z[g])
                if g >= 2:
                    act.wait(s_one, n_one2[g - 2])
                n_gate[g] = act.do(lambda e: e.activation(gate[:, sl, 0:m], zed[:, sl, 0:m], ACT.Sigmoid, bias=b2[:, 0:1]), s_gate)

            n_one2 = {}

            def weigh(g):
                m, sl = tiles[g], g % NONE
                dve.wait(s_gate, n_gate[g])
                dve.wait(s_one, n_one[g])
                o = oneh[:, sl, 0:m, :]
                n_one[g] = dve.do(lambda e: e.tensor_tensor(
                    out=o, in0=o, in1=gate[:, g % 2, 0:m].unsqueeze(2).to_broadcast([P, m, WIN]), op=ALU.mult), s_one)
                n_one2[g] = n_one[g]

            dve.wait(s_zero, n_zero)
            if layer != 1:
                for g in range(ng):
                    gather(g)
                    onehot(g)
                    scatter(g)
                    if g >= 1:
                        accumulate(g - 1)
                accumulate(ng - 1)
            else:
                for g in range(ng + 3):
                    if 2 <= g <= ng + 1:
                        weigh(g - 2)
                        scatter(g - 2)
                    if g < ng:
                        gather(g)
                        fetch_window(g)
                        onehot_t(g)
                        onehot(g)
                        spread(g)
                    if 1 <= g <= ng:
                        logits(g - 1)
                    if 3 <= g:
                        accumulate(g - 3)
            general(layer, table, idx, width, feat, sums)

        def general(layer, table, idx, width, feat, sums):
            q = gen_sems[layer]
            rowbuf = rows[:, 0, :, :]
            one = rows[:, 1, :, 0:P]
            prow = rows[:, 1, :, P:2 * P]
            bank = ps_a[0]

            def guarded(body):
                def run(eng):
                    flag = eng.value_load(outside[0:1, 0:1], min_val=0, max_val=n_edges)
                    with eng.If(flag):
                        body(eng)
                return run

            def on_dve(e):
                with e.Fori(0, ng) as g:
                    cols = bass.ds(g * TPG, TPG)
                    rel = dst_rel[:, cols]
                    e.tensor_copy(gen_idx[:, :], idx[:, cols])
                    if layer == 3:
                        e.tensor_copy(gen_wt[:, :], wt[:, cols])
                    e.tensor_scalar(gen_in[:, :], rel, 0.0, None, ALU.is_ge)
                    e.tensor_scalar(gen_abs[:, :], rel, win_node[:, bass.ds(g, 1)], None, ALU.add)
                    e.drain()
                    e.scalar_tensor_tensor(out=gen_in[:, :], in0=rel, scalar=float(WIN), in1=gen_in[:, :],
                                           op0=ALU.is_lt, op1=ALU.mult)
                    e.tensor_scalar(gen_abs[:, :], gen_abs[:, :], iota_p[:, 0:1], None, ALU.subtract)
                    e.drain()
                    e.scalar_tensor_tensor(out=gen_dst[:, :], in0=gen_in[:, :], scalar=-4.0 * npad, in1=gen_abs[:, :],
                                           op0=ALU.mult, op1=ALU.add)
                    e.tensor_scalar(gen_tgt[:, :], gen_abs[:, :], 0.0, None, ALU.max)
                    e.drain().then_inc(q["idx"], 1)
                    if layer == 1:
                        e.wait_ge(q["row"], (g + 1) * (16 * TPG))
                        e.wait_ge(q["prow"], (g + 1) * (16 * TPG))
                        dd = diff[:, 0, :, :]
                        e.tensor_tensor(out=dd, in0=prow, in1=rowbuf[:, :, 0:P], op=ALU.subtract)
                        e.drain()
                        e.scalar_tensor_tensor(out=dd, in0=dd, scalar=0.0, in1=bcast(w2, TPG), op0=ALU.max, op1=ALU.mult)
                        e.drain()
                        e.tensor_reduce(out=zed[:, 0, :], in_=dd, axis=AXX, op=ALU.add).then_inc(q["z"], 1)
                        e.wait_ge(q["gate"], g + 1)
                        e.tensor_copy(gen_wt[:, :], gate[:, 0, :])
                        e.drain()
                    with e.Fori(0, nb) as b:
                        done = g * nb + b
                        e.tensor_tensor(out=one, in0=iota_b[:, :].unsqueeze(1).to_broadcast([P, TPG, P]),
                                        in1=gen_dst[:, :].unsqueeze(2).to_broadcast([P, TPG, P]), op=ALU.is_equal)
                        e.drain()
                        e.tensor_scalar(gen_dst[:, :], gen_dst[:, :], float(P), None, ALU.subtract)
                        if layer in (1, 3):
                            e.tensor_tensor(out=one, in0=one, in1=gen_wt[:, :].unsqueeze(2).to_broadcast([P, TPG, P]),
                                            op=ALU.mult)
                        e.drain().then_inc(q["one"], 1)
                        e.wait_ge(q["scat"], done + 1)
                        a = acc[:, 0:sums, bass.ds(b * P, P)]
                        v = bank[:, 0:sums * P].rearrange("p (k w) -> p k w", k=sums)
                        e.tensor_tensor(out=a, in0=a, in1=v, op=ALU.add)
                        e.drain()

            def on_pool(e):
                with e.Fori(0, ng) as g:
                    e.wait_ge(q["idx"], g + 1)
                    e.sem_inc(q["seen"])
                    for t in range(TPG):
                        e.indirect_dma_start(out=rowbuf[:, t, 0:width], out_offset=None, in_=table[:, :],
                                             in_offset=bass.IndirectOffsetOnAxis(ap=gen_idx[:, t:t + 1], axis=0)
                                             ).then_inc(q["row"], 16)
                    for t in range(TPG if layer == 1 else 0):
                        e.indirect_dma_start(out=prow[:, t, :], out_offset=None, in_=tab_pb[:, :],
                                             in_offset=bass.IndirectOffsetOnAxis(ap=gen_tgt[:, t:t + 1], axis=0)
                                             ).then_inc(q["prow"], 16)

            def on_act(e):
                with e.Fori(0, ng) as g:
                    e.wait_ge(q["z"], g + 1)
                    e.activation(gate[:, 0, :], zed[:, 0, :], ACT.Sigmoid, bias=b2[:, 0:1]).then_inc(q["gate"], 1)

            def on_pe(e):
                with e.Fori(0, ng) as g:
                    e.wait_ge(q["row"], (g + 1) * (16 * TPG))
                    e.sem_inc(q["seen"])
                    with e.Fori(0, nb) as b:
                        e.wait_ge(q["one"], g * nb + b + 1)
                        for t in range(TPG):
                            last = e.matmul(bank[:, 0:P], rowbuf[:, t, feat], one[:, t, :], start=t == 0, stop=t == TPG - 1)
                        for t in range(TPG if sums == 2 else 0):
                            last = e.matmul(bank[:, P:2 * P], ones[:, :], one[:, t, :], start=t == 0, stop=t == TPG - 1)
                        last.then_inc(q["scat"], 1)

            dve.wait(s_add, s_add.value)
            dve.do(guarded(on_dve))
            pool.do(guarded(on_pool))
            pe.do(guarded(on_pe))
            if layer == 1:
                act.do(guarded(on_act))
            dve.do(lambda e: e.drain(), s_gen)

        acc_read = []

        def ones_sums(keep):
            pe.wait(s_gen, s_gen.value)
            wait_free(pe, "ps_t0")
            for b in range(nb):
                f = lambda e, b=b: e.matmul(ps_t[0][:, b:b + 1], acc[0:1, 1, b * P:(b + 1) * P], ones[0:1, 0:1], start=True, stop=True)
                n = pe.do(f, s_cnt) if b == nb - 1 else pe.do(f)
            dve.wait(s_cnt, n)
            if keep == "degree":
                n = dve.do(lambda e: e.tensor_copy(indeg[:, :], ps_t[0][:, 0:nb]), s_node)
                dve.wait(s_node, n)
                n = dve.do(lambda e: e.tensor_scalar(rdeg[:, :], indeg[:, :], 1.0, None, ALU.max), s_node)
                dve.wait(s_node, n)
                n = dve.do(lambda e: e.reciprocal(rdeg[:, :], rdeg[:, :]), s_node)
            else:
                n = dve.do(lambda e: e.tensor_copy(sumw[:, :], ps_t[0][:, 0:nb]), s_node)
            dve.wait(s_node, n)
            node_free["ps_t0"] = [(s_node, n)]

        for i, (c, m) in enumerate(chunks):
            node_pre(0, i, c, m)
        for layer in range(4):
            edges(layer, n_zero)
            if layer < 2:
                ones_sums(("degree", "gates")[layer])
                node_free["sums_read"] = [(s_cnt, s_cnt.value)]
            for i, (c, m) in enumerate(chunks):
                node_post(layer, i, c, m, [(s_add, s_add.value), (s_gen, s_gen.value)])
                if layer < 3:
                    pool.wait(s_mm, acc_read[-1])
                    halves = 2 if layer == 0 else 1
                    if halves == 2:
                        pool.wait(s_cnt, s_cnt.value)
                    n_zero = pool.do(lambda e, c=c, m=m, halves=halves: e.memset(acc[:, 0:halves, c * P:(c + m) * P], 0.0), s_zero)
                    node_pre(layer + 1, i, c, m)
        sp.wait(s_out, s_out.value)

        block = ctx.enter_context(nc.Block())
        block.sync(lambda eng: sp.emit(eng))
        block.gpsimd(lambda eng: pool.emit(eng))
        block.scalar(lambda eng: act.emit(eng))
        block.vector(lambda eng: dve.emit(eng))
        block.tensor(lambda eng: pe.emit(eng))


_INS = ["x", "src", "dst", "edge_type_8", "edge_weight1", "L0_gnn_W", "L0_gnn_b", "L1_gnn_W1", "L1_gnn_b1",
        "L1_gnn_W2", "L1_gnn_b2", "L1_gnn_W4", "L1_gnn_b4", "L2_gnn_Wp", "L2_gnn_bp", "L2_gnn_Wl", "L2_gnn_bl",
        "L2_gnn_Wr", "L3_gnn_weight", "L3_gnn_loop_weight"]


def kernel(**inputs):
    import numpy as np
    import concourse.bacc as bacc
    from concourse.bass_utils import run_bass_kernel_spmd

    nc = bacc.Bacc("TRN2", target_bir_lowering=False, num_devices=1)
    arrays, args = {}, {}
    for name in _INS:
        a = np.ascontiguousarray(inputs[name])
        arrays["in_" + name] = a
        args[name] = nc.dram_tensor("in_" + name, a.shape, mybir.dt.from_np(a.dtype), kind="ExternalInput").ap()
    out = nc.dram_tensor("out_x", args["x"].shape, F32, kind="ExternalOutput").ap()
    gnn_program(nc, args, out)
    r = run_bass_kernel_spmd(nc, [arrays], core_ids=[0])
    return r.results[0]["out_x"]
```

```python
import concourse.bass as bass
from concourse import mybir
from concourse.alu_op_type import AluOpType as ALU
from contextlib import ExitStack

ACT = mybir.ActivationFunctionType
AXX = mybir.AxisListType.X
F32, I32, U32 = mybir.dt.float32, mybir.dt.int32, mybir.dt.uint32

P = 128
TPG = 4
WIN = 64
CH = 4
NSLOT = 11
NONE = 3
EPS_LN, EPS_NORM = 1e-5, 1e-12


class Sem:

    def __init__(self, handle):
        self.handle, self.value = handle, 0


class Queue:

    def __init__(self):
        self.items = []

    def do(self, make, sem=None, by=1):
        if sem is None:
            self.items.append(lambda eng: make(eng))
            return None
        sem.value += by
        self.items.append(lambda eng: make(eng).then_inc(sem.handle, by))
        return sem.value

    def dma(self, make, sem):
        return self.do(make, sem, 16)

    def wait(self, sem, value):
        if value:
            self.items.append(lambda eng: eng.wait_ge(sem.handle, value))

    def emit(self, eng):
        for item in self.items:
            item(eng)


def gnn_program(nc, ins, out):
    x_in = ins["x"]
    n_nodes, d = x_in.shape
    n_edges = ins["src"].shape[0]
    n_rel = ins["L3_gnn_weight"].shape[0]
    assert d == P
    nb = -(-n_nodes // P)
    npad = nb * P
    nt = -(-n_edges // P)
    ng = -(-nt // TPG)
    nr = -(-nt // P)
    chunks = [(c, min(CH, nb - c)) for c in range(0, nb, CH)]
    full_tiles = n_edges // P
    rest_edges = n_edges - full_tiles * P
    last_rows = n_nodes - (nb - 1) * P

    with ExitStack() as ctx:
        def sb(name, shape, dt=F32):
            return ctx.enter_context(nc.sbuf_tensor(name, shape, dt))

        def sem(name):
            return Sem(ctx.enter_context(nc.semaphore(name)))

        def dram(name, shape, dt=F32):
            return nc.dram_tensor(name, shape, dt, kind="Internal").ap()

        tab_h = [dram(f"tab_h{i}", (npad, P)) for i in range(2)]
        tab_p = dram("tab_p", (npad, P))
        tab_m = dram("tab_m", (npad, P))
        tab_rel = dram("tab_rel", (npad * n_rel, P))
        dst_flat = dram("dst_flat", (nr * P * P,))

        x = sb("x", [P, nb, P])
        h = sb("h", [P, nb, P])
        acc = sb("acc", [P, 2, npad])
        rself = acc[:, 1, :].rearrange("p (b f) -> p b f", f=P)
        rows = sb("rows", [P, NSLOT, TPG, P])
        spare = rows[:, :, :, :].rearrange("p a b c -> p (a b c)")
        stage = spare[:, 0:2 * CH * P].rearrange("p (s b f) -> p s b f", s=2, f=P)
        stage2 = spare[:, 2 * CH * P:4 * CH * P].rearrange("p (s b f) -> p s b f", s=2, f=P)
        stage_rel = spare[:, 0:3 * n_rel * P].rearrange("p (s f) -> p s f", s=3)
        raw = acc[:, :, :].rearrange("p k n -> p (k n)")
        idx_src = sb("idx_src", [P, nr * P], U32)
        idx_rel = sb("idx_rel", [P, nr * P], U32)
        dst_rel = sb("dst_rel", [P, nr * P])
        wt = sb("wt", [P, nr * P])
        win_node = sb("win_node", [P, ng])
        base_row = sb("base_row", [1, ng])
        base_int = sb("base_int", [1, ng], I32)
        oneh = sb("oneh", [P, NONE, TPG, WIN])
        onehT = sb("onehT", [WIN, 2, TPG * P])
        dst_bc = sb("dst_bc", [WIN, 3, TPG * P])
        pwin = sb("pwin", [WIN, 3, P])
        hid = sb("hid", [P, 2, TPG * P])
        zed = sb("zed", [P, TPG])
        b1col = sb("b1col", [P, 1])
        w2col = sb("w2col", [P, 1])
        w1neg = sb("w1neg", [P, P])
        nmr = sb("nmr", [P, nb])
        gate = sb("gate", [P, 2, TPG])
        hT = sb("hT", [P, 2, CH * P])
        stats = sb("stats", [P, nb, 6])
        mv = sb("mv", [P, nb, 2])
        std = sb("std", [P, nb])
        rstd = sb("rstd", [P, nb])
        indeg = sb("indeg", [P, nb])
        rdeg = sb("rdeg", [P, nb])
        sumw = sb("sumw", [P, nb])
        tmp = sb("tmp", [P, 2, CH, P])
        tmp2 = sb("tmp2", [P, 2, CH, P])
        nrm = sb("nrm", [P, nb])
        ident = sb("ident", [P, P])
        ones = sb("ones", [P, P])
        iota_b = sb("iota_b", [P, P])
        iota_w = iota_b[:, 0:WIN]
        iota_p = sb("iota_p", [P, 1])
        eps_ln = sb("eps_ln", [P, 1])
        b2 = sb("b2", [P, 1])
        w0 = sb("w0", [P, 2 * P])
        w0a, w0b = sb("w0a", [P, P]), sb("w0b", [P, P])
        w1, w4 = sb("w1", [P, P]), sb("w4", [P, P])
        wp, wl, wr = sb("wp", [P, P]), sb("wl", [P, P]), sb("wr", [P, P])
        wpT, wlT, wrT = sb("wpT", [P, P]), sb("wlT", [P, P]), sb("wrT", [P, P])
        wrel = sb("wrel", [P, n_rel * P])
        wloop = sb("wloop", [P, P])
        bias0, bias1, bias4, biasp, biasl, w2 = (sb(n, [P, P]) for n in ("bias0", "bias1", "bias4", "biasp", "biasl", "w2"))
        n_inside = sb("n_inside", [P, 1])
        outside = sb("outside", [1, 1], I32)
        gen_idx = sb("gen_idx", [P, TPG], U32)
        gen_tgt = sb("gen_tgt", [P, TPG], U32)
        gen_dst = sb("gen_dst", [P, TPG])
        gen_abs = sb("gen_abs", [P, TPG])
        gen_in = sb("gen_in", [P, TPG])
        gen_wt = sb("gen_wt", [P, TPG])

        ps = [ctx.enter_context(nc.psum_tensor(f"ps{i}", [P, 512], F32)) for i in range(8)]
        ps_t, ps_m, ps_e, ps_a = ps[0:2], ps[2:4], ps[4:6], ps[6:8]

        s_const = sem("s_const")
        s_win = sem("s_win")
        s_wgt = sem("s_wgt")
        s_xin = [sem(f"s_xin{i}") for i in range(len(chunks))]
        s_pad = sem("s_pad")
        s_prep = sem("s_prep")
        s_prepT = sem("s_prepT")
        s_dstf = sem("s_dstf")
        s_ln = sem("s_ln")
        s_sqrt = sem("s_sqrt")
        s_h = sem("s_h")
        s_tr = sem("s_tr")
        s_hT = sem("s_hT")
        s_mm = sem("s_mm")
        s_node = sem("s_node")
        s_relu = sem("s_relu")
        s_tab = [sem(f"s_tab{i}") for i in range(3)]
        s_tabh = sem("s_tabh")
        s_zero = sem("s_zero")
        s_row = [sem(f"s_row{i}") for i in range(NSLOT)]
        s_one = sem("s_one")
        s_scat = sem("s_scat")
        s_add = sem("s_add")
        s_bc = [sem(f"s_bc{i}") for i in range(3)]
        s_pw = [sem(f"s_pw{i}") for i in range(3)]
        s_oneT = sem("s_oneT")
        s_rowT = sem("s_rowT")
        s_gT = sem("s_gT")
        s_hid = sem("s_hid")
        s_act = sem("s_act")
        s_z = sem("s_z")
        s_gate = sem("s_gate")
        s_cnt = sem("s_cnt")
        s_out = sem("s_out")
        s_gen = sem("s_gen")
        gen_sems = [{k: ctx.enter_context(nc.semaphore(f"g{layer}_{k}")) for k in
                     ("idx", "row", "prow", "z", "gate", "one", "scat", "seen")} for layer in range(4)]

        pe, dve, act, pool, sp = (Queue() for _ in range(5))

        pool.do(lambda e: e.memset(ident[:, :], 0.0), s_const)
        pool.do(lambda e: e.memset(ones[:, :], 1.0), s_const)
        pool.do(lambda e: e.memset(eps_ln[:, :], EPS_LN), s_const)
        pool.do(lambda e: e.iota(iota_b[:, :], [[1, P]], base=0, channel_multiplier=0,
                                 allow_small_or_imprecise_dtypes=True), s_const)
        n = pool.do(lambda e: e.iota(iota_p[:, :], [[1, 1]], base=0, channel_multiplier=1,
                                     allow_small_or_imprecise_dtypes=True), s_const)
        pool.wait(s_const, n)
        n_const = pool.do(lambda e: e.affine_select(
            out=ident[:, :], in_=ident[:, :], compare_op=ALU.not_equal, fill=1.0,
            base=0, pattern=[[-1, P]], channel_multiplier=1), s_const)

        rblk = nr * P
        raw_src = raw[:, 0 * rblk:1 * rblk].bitcast(I32)
        raw_dst = raw[:, 1 * rblk:2 * rblk].bitcast(I32)
        raw_typ = raw[:, 2 * rblk:3 * rblk].bitcast(I32)
        raw_wt = raw[:, 3 * rblk:4 * rblk]
        f_src, f_dst, f_rel = (spare[:, i * rblk:(i + 1) * rblk] for i in range(3))
        assert 4 * rblk <= 2 * npad and 3 * rblk <= NSLOT * TPG * P
        body = (nr - 1) * P
        tail = full_tiles - body
        pads = ((raw_src, 0), (raw_dst, -1), (raw_typ, 0), (raw_wt, 0))
        dve.do(lambda e: e.memset(x[:, nb - 1, :], 0.0), s_pad)
        for v, fill in pads:
            n_pad = dve.do(lambda e, v=v, fill=fill: e.memset(v[:, body:rblk], fill), s_pad)
        sp.wait(s_pad, n_pad)
        for i, (c, m) in enumerate(chunks):
            full = m - 1 if c + m == nb else m
            if full:
                sp.dma(lambda e, c=c, full=full: e.dma_start(
                    x[:, c:c + full, :], x_in[c * P:(c + full) * P, :].rearrange("(b p) f -> p b f", p=P)), s_xin[i])
            if c + m == nb:
                sp.dma(lambda e: e.dma_start(x[0:last_rows, nb - 1, :], x_in[(nb - 1) * P:n_nodes, :]), s_xin[i])
        for name, v in (("src", raw_src), ("dst", raw_dst), ("edge_type_8", raw_typ), ("edge_weight1", raw_wt)):
            a = ins[name]
            if len(a.shape) == 2:
                a = a.rearrange("n o -> (n o)")
            v3 = v.rearrange("p (b e) -> p b e", e=P)
            sp.dma(lambda e, a=a, v3=v3: e.dma_start(
                v3[:, 0:nr - 1, :], a[0:body * P].rearrange("(b p e) -> p b e", p=P, e=P)), s_win)
            sp.dma(lambda e, a=a, v3=v3: e.dma_start(
                v3[0:tail, nr - 1, :], a[body * P:full_tiles * P].rearrange("(p e) -> p e", e=P)), s_win)
            if rest_edges:
                n_win = sp.dma(lambda e, a=a, v3=v3: e.dma_start(
                    v3[tail:tail + 1, nr - 1, 0:rest_edges],
                    a[full_tiles * P:n_edges].rearrange("(p e) -> p e", p=1)), s_win)
        n_win = s_win.value
        for t, a in ((w0, ins["L0_gnn_W"]), (w1, ins["L1_gnn_W1"]), (w4, ins["L1_gnn_W4"]), (wp, ins["L2_gnn_Wp"]),
                     (wl, ins["L2_gnn_Wl"]), (wr, ins["L2_gnn_Wr"]), (wloop, ins["L3_gnn_loop_weight"])):
            act.dma(lambda e, t=t, a=a: e.dma_start(t[:, :], a), s_wgt)
        act.dma(lambda e: e.dma_start(wrel[:, :].rearrange("p (r o) -> p r o", r=n_rel),
                                      ins["L3_gnn_weight"].rearrange("r i o -> i r o")), s_wgt)
        for t, a in ((bias0, ins["L0_gnn_b"]), (bias1, ins["L1_gnn_b1"]), (bias4, ins["L1_gnn_b4"]),
                     (biasp, ins["L2_gnn_bp"]), (biasl, ins["L2_gnn_bl"]),
                     (w2, ins["L1_gnn_W2"].rearrange("n o -> (n o)")), (b2, ins["L1_gnn_b2"])):
            act.dma(lambda e, t=t, a=a: e.dma_start(t[:, :], a.partition_broadcast(P)), s_wgt)
        act.dma(lambda e: e.dma_start(b1col[:, :], ins["L1_gnn_b1"].rearrange("(p o) -> p o", o=1)), s_wgt)
        act.dma(lambda e: e.dma_start(w2col[:, :], ins["L1_gnn_W2"]), s_wgt)
        n_wgt = s_wgt.value

        pe.wait(s_const, n_const)
        dve.wait(s_const, n_const)
        act.wait(s_const, n_const)
        pe.wait(s_wgt, n_wgt)
        for srcv, dstv in ((w0[:, 0:P], w0a), (w0[:, P:2 * P], w0b), (wp[:, :], wpT), (wl[:, :], wlT), (wr[:, :], wrT)):
            pe.wait(s_prep, s_prep.value)
            n = pe.do(lambda e, srcv=srcv: e.transpose(ps_t[1][:, 0:P], srcv, ident[:, :]), s_prepT)
            dve.wait(s_prepT, n)
            dve.do(lambda e, dstv=dstv: e.tensor_copy(dstv[:, :], ps_t[1][:, 0:P]), s_prep)
        dve.wait(s_wgt, n_wgt)
        act.wait(s_wgt, n_wgt)
        n_w = dve.do(lambda e: e.tensor_scalar(w1neg[:, :], w1[:, :], -1.0, None, ALU.mult), s_prep)
        pe.wait(s_prep, n_w)

        st = {"bank": 0}
        node_free = {}
        x_ready = {}

        def wait_free(q, key):
            for s, v in node_free.get(key, ()):
                q.wait(s, v)

        def layernorm(layer, i, c, m, res):
            if layer == 0:
                dve.wait(s_xin[i], s_xin[i].value)
                act.wait(s_xin[i], s_xin[i].value)
            dve.wait(s_node, x_ready.get(c, 0))
            for b in range(c, c + m):
                n = dve.do(lambda e, b=b: e.bn_stats(stats[:, b, :], x[:, b, :]), s_ln)
            dve.wait(s_ln, n)
            for b in range(c, c + m):
                n = dve.do(lambda e, b=b: e.bn_aggr(mv[:, b, :], stats[:, b, :]), s_ln)
            act.wait(s_ln, n)
            n_std = act.do(lambda e: e.activation(std[:, c:c + m], mv[:, c:c + m, 1], ACT.Sqrt, bias=eps_ln[:, 0:1]), s_sqrt)
            yield
            dve.wait(s_sqrt, n_std)
            n = dve.do(lambda e: e.reciprocal(rstd[:, c:c + m], std[:, c:c + m]), s_ln)
            dve.wait(s_ln, n)
            n = dve.do(lambda e: e.scalar_tensor_tensor(out=nmr[:, c:c + m], in0=mv[:, c:c + m, 0], scalar=-1.0,
                                                        in1=rstd[:, c:c + m], op0=ALU.mult, op1=ALU.mult), s_ln)
            act.wait(s_ln, n)
            act.wait(s_node, x_ready.get(c, 0))
            wait_free(act, "h%d" % c)
            for b in range(c, c + m):
                n = act.do(lambda e, b=b: e.activation(h[:, b, :], x[:, b, :], ACT.Relu, bias=nmr[:, b:b + 1],
                                                       scale=rstd[:, b:b + 1]), s_h)
            node_free["x%d" % c] = [(s_h, n)]
            res["h"] = n

        def transposed(blocks, ready, slot):
            bank = ps_t[slot]
            for s, v in ready:
                pe.wait(s, v)
            wait_free(pe, "ps_t%d" % slot)
            for j, blk in enumerate(blocks):
                f = lambda e, j=j, blk=blk: e.transpose(bank[:, j * P:(j + 1) * P], blk, ident[:, :])
                n = pe.do(f, s_tr) if j == len(blocks) - 1 else pe.do(f)
            act.wait(s_tr, n)
            wait_free(act, "hT%d" % slot)
            m = len(blocks)
            n = act.do(lambda e: e.copy(hT[:, slot, 0:m * P], bank[:, 0:m * P]), s_hT)
            node_free["ps_t%d" % slot] = [(s_hT, n)]
            return n

        def product(slot, m, weight, ready):
            k = st["bank"] % 2
            st["bank"] += 1
            bank, key = ps_m[k], "ps_m%d" % k
            for s, v in ready:
                pe.wait(s, v)
            wait_free(pe, key)
            for j in range(m):
                f = lambda e, j=j: e.matmul(bank[:, j * P:(j + 1) * P], hT[:, slot, j * P:(j + 1) * P], weight[:, :],
                                            start=True, stop=True)
                n = pe.do(f, s_mm) if j == m - 1 else pe.do(f)
            return bank[:, 0:m * P].rearrange("p (b f) -> p b f", f=P), n, key

        def bcast(v, m):
            return v[:, :].unsqueeze(1).to_broadcast([P, m, P])

        def xadd(c, m, make):
            dve.wait(s_node, x_ready.get(c, 0))
            wait_free(dve, "x%d" % c)
            x_ready[c] = dve.do(make, s_node)
            return x_ready[c]

        tab_done = {}

        def table_write(make, s):
            n = sp.dma(make, s)
            tab_done[s] = n
            return n

        def rows_of(tab, c, m):
            return tab[c * P:(c + m) * P, :].rearrange("(b p) f -> p b f", p=P)

        def self_term(layer, c, m, slot, n_h, n_hT):
            xc = x[:, c:c + m, :]
            if layer == 0:
                v, n, key = product(slot, m, w0a, [(s_hT, n_hT)])
                node_free["hT%d" % slot] = [(s_mm, n)]
                dve.wait(s_mm, n)
                n = xadd(c, m, lambda e: e.tensor_tensor(out=xc, in0=v, in1=xc, op=ALU.add))
                node_free[key] = [(s_node, n)]
                xadd(c, m, lambda e: e.tensor_tensor(out=xc, in0=xc, in1=bcast(bias0, m), op=ALU.add))
            elif layer == 1:
                v, n, key = product(slot, m, w4, [(s_hT, n_hT)])
                node_free["hT%d" % slot] = [(s_mm, n)]
                dve.wait(s_mm, n)
                wait_free(dve, "tmp%d" % slot)
                n = dve.do(lambda e: e.tensor_tensor(out=tmp[:, slot, 0:m, :], in0=v, in1=bcast(bias4, m), op=ALU.add), s_node)
                node_free[key] = [(s_node, n)]
                dve.wait(s_node, n)
                dve.wait(s_node, x_ready.get(c, 0))
                wait_free(dve, "x%d" % c)
                for j in range(m):
                    n = dve.do(lambda e, j=j: e.scalar_tensor_tensor(
                        out=x[:, c + j, :], in0=tmp[:, slot, j, :], scalar=indeg[:, c + j:c + j + 1],
                        in1=x[:, c + j, :], op0=ALU.mult, op1=ALU.add), s_node)
                x_ready[c] = n
                node_free["tmp%d" % slot] = [(s_node, n)]
            elif layer == 2:
                v, n, key = product(slot, m, wrT, [(s_hT, n_hT)])
                node_free["hT%d" % slot] = [(s_mm, n)]
                dve.wait(s_mm, n)
                wait_free(dve, "sums_read")
                n = dve.do(lambda e: e.tensor_tensor(out=rself[:, c:c + m, :], in0=v, in1=bcast(biasl, m), op=ALU.add), s_node)
                node_free[key] = [(s_node, n)]
                dve.wait(s_h, n_h)
                n = xadd(c, m, lambda e: e.tensor_tensor(out=xc, in0=xc, in1=h[:, c:c + m, :], op=ALU.add))
                node_free["h%d" % c] = [(s_node, n)]
            else:
                v, n, key = product(slot, m, wloop, [(s_hT, n_hT)])
                node_free["hT%d" % slot] = [(s_mm, n)]
                dve.wait(s_mm, n)
                n = xadd(c, m, lambda e: e.tensor_tensor(out=xc, in0=v, in1=xc, op=ALU.add))
                node_free[key] = [(s_node, n)]

        def node_pre(layer, i, c, m):
            res = {}
            yield from layernorm(layer, i, c, m, res)
            n_h = res["h"]
            slot = i % 2
            hc = h[:, c:c + m, :]
            if layer < 2:
                sp.wait(s_h, n_h)
                table_write(lambda e: e.dma_start(rows_of(tab_h[layer], c, m), hc), s_tabh)
            yield
            n_hT = transposed([h[:, b, :] for b in range(c, c + m)], [(s_h, n_h)], slot)
            node_free["h%d" % c] = [(s_tr, s_tr.value)]
            pe_ready = [(s_hT, n_hT)]
            yield
            if layer == 1:
                v, n, key = product(slot, m, w1, pe_ready)
                act.wait(s_mm, n)
                wait_free(act, "stage%d" % slot)
                na = act.do(lambda e: e.copy(stage[:, slot, 0:m, :], v), s_relu)
                node_free[key] = [(s_relu, na)]
                sp.wait(s_relu, na)
                nt_ = table_write(lambda e: e.dma_start(rows_of(tab_p, c, m), stage[:, slot, 0:m, :]), s_tab[slot])
                node_free["stage%d" % slot] = [(s_tab[slot], nt_)]
            elif layer == 2:
                v, n, key = product(slot, m, wpT, pe_ready)
                dve.wait(s_mm, n)
                wait_free(dve, "stage2%d" % slot)
                nd = dve.do(lambda e: e.tensor_tensor(out=stage2[:, slot, 0:m, :], in0=v, in1=bcast(biasp, m), op=ALU.add), s_node)
                node_free[key] = [(s_node, nd)]
                act.wait(s_node, nd)
                wait_free(act, "stage%d" % slot)
                na = act.do(lambda e: e.activation(stage[:, slot, 0:m, :], stage2[:, slot, 0:m, :], ACT.Relu), s_relu)
                node_free["stage2%d" % slot] = [(s_relu, na)]
                sp.wait(s_relu, na)
                nt_ = table_write(lambda e: e.dma_start(rows_of(tab_m, c, m), stage[:, slot, 0:m, :]), s_tab[slot])
                node_free["stage%d" % slot] = [(s_tab[slot], nt_)]
            elif layer == 3:
                half = n_rel * P // 2
                rel_rows = tab_rel.rearrange("(n r) f -> n (r f)", r=n_rel)
                for j in range(m):
                    b = c + j
                    sl = b % 3
                    wait_free(act, "rel%d" % sl)
                    wait_free(dve, "rel%d" % sl)
                    for part in range(2):
                        k = st["bank"] % 2
                        st["bank"] += 1
                        bank, key = ps_m[k], "ps_m%d" % k
                        pe.wait(s_hT, n_hT)
                        wait_free(pe, key)
                        n = pe.do(lambda e, j=j, part=part, bank=bank: e.matmul(
                            bank[:, 0:half], hT[:, slot, j * P:(j + 1) * P], wrel[:, part * half:(part + 1) * half],
                            start=True, stop=True), s_mm)
                        dstv = stage_rel[:, sl, part * half:(part + 1) * half]
                        if part == 0:
                            act.wait(s_mm, n)
                            na = act.do(lambda e, bank=bank, dstv=dstv: e.copy(dstv, bank[:, 0:half]), s_relu)
                            node_free[key] = [(s_relu, na)]
                        else:
                            dve.wait(s_mm, n)
                            nd = dve.do(lambda e, bank=bank, dstv=dstv: e.tensor_copy(dstv, bank[:, 0:half]), s_node)
                            node_free[key] = [(s_node, nd)]
                    sp.wait(s_relu, na)
                    sp.wait(s_node, nd)
                    nt_ = table_write(lambda e, b=b, sl=sl: e.dma_start(rel_rows[b * P:(b + 1) * P, :], stage_rel[:, sl, :]), s_tab[sl])
                    node_free["rel%d" % sl] = [(s_tab[sl], nt_)]
            self_term(layer, c, m, slot, n_h, n_hT)

        def node_post(layer, i, c, m, ready):
            xc = x[:, c:c + m, :]
            cols = [acc[:, 0, b * P:(b + 1) * P] for b in range(c, c + m)]
            k = st["bank"] % 2
            st["bank"] += 1
            bank, key = ps_m[k], "ps_m%d" % k
            for s, v in ready:
                pe.wait(s, v)
            wait_free(pe, key)
            weight = {0: w0b, 2: wlT}.get(layer)
            for j in range(m):
                if weight is None:
                    f = lambda e, j=j: e.transpose(bank[:, j * P:(j + 1) * P], cols[j], ident[:, :])
                else:
                    f = lambda e, j=j: e.matmul(bank[:, j * P:(j + 1) * P], cols[j], weight[:, :], start=True, stop=True)
                n = pe.do(f, s_mm) if j == m - 1 else pe.do(f)
            v = bank[:, 0:m * P].rearrange("p (b f) -> p b f", f=P)
            if layer < 3:
                pool.wait(s_mm, n)
                pool.wait(s_cnt, s_cnt.value)
                halves = 2 if layer == 0 else 1
                pool.do(lambda e: e.memset(acc[:, 0:halves, c * P:(c + m) * P], 0.0), s_zero)
            slot = i % 2
            dve.wait(s_mm, n)
            if layer == 0:
                dve.wait(s_node, x_ready[c])
                for j in range(m):
                    n = dve.do(lambda e, j=j: e.scalar_tensor_tensor(
                        out=x[:, c + j, :], in0=v[:, j, :], scalar=rdeg[:, c + j:c + j + 1], in1=x[:, c + j, :],
                        op0=ALU.mult, op1=ALU.add), s_node)
                x_ready[c] = n
                node_free[key] = [(s_node, n)]
            elif layer == 1:
                dve.wait(s_node, x_ready[c])
                for j in range(m):
                    n = dve.do(lambda e, j=j: e.scalar_tensor_tensor(
                        out=x[:, c + j, :], in0=h[:, c + j, :], scalar=sumw[:, c + j:c + j + 1], in1=x[:, c + j, :],
                        op0=ALU.mult, op1=ALU.add), s_node)
                x_ready[c] = n
                n = xadd(c, m, lambda e: e.tensor_tensor(out=xc, in0=xc, in1=v, op=ALU.subtract))
                node_free[key] = [(s_node, n)]
                node_free["h%d" % c] = node_free["h%d" % c] + [(s_node, n)]
            elif layer == 2:
                o, o2 = tmp[:, slot, 0:m, :], tmp2[:, slot, 0:m, :]
                wait_free(dve, "tmp%d" % slot)
                for j in range(m):
                    n = dve.do(lambda e, j=j: e.scalar_tensor_tensor(
                        out=o[:, j, :], in0=v[:, j, :], scalar=rdeg[:, c + j:c + j + 1], in1=rself[:, c + j, :],
                        op0=ALU.mult, op1=ALU.add), s_node)
                node_free[key] = [(s_node, n)]
                dve.wait(s_node, n)
                n = dve.do(lambda e: e.tensor_scalar(o2, o, 0.0, None, ALU.min), s_node)
                yield
                act.wait(s_node, n)
                na = act.do(lambda e: e.activation(o2, o2, ACT.Exp), s_relu)
                n = dve.do(lambda e: e.tensor_scalar(o, o, 0.0, None, ALU.max), s_node)
                dve.wait(s_node, n)
                dve.wait(s_relu, na)
                n = dve.do(lambda e: e.scalar_tensor_tensor(out=o, in0=o2, scalar=-1.0, in1=o, op0=ALU.add, op1=ALU.add), s_node)
                dve.wait(s_node, n)
                n = dve.do(lambda e: e.tensor_tensor(out=o2, in0=o, in1=o, op=ALU.mult), s_node)
                dve.wait(s_node, n)
                n = dve.do(lambda e: e.tensor_reduce(out=nrm[:, c:c + m], in_=o2, axis=AXX, op=ALU.add), s_node)
                yield
                act.wait(s_node, n)
                na = act.do(lambda e: e.activation(nrm[:, c:c + m], nrm[:, c:c + m], ACT.Sqrt), s_relu)
                dve.wait(s_relu, na)
                n = dve.do(lambda e: e.tensor_scalar(nrm[:, c:c + m], nrm[:, c:c + m], EPS_NORM, None, ALU.max), s_node)
                dve.wait(s_node, n)
                n = dve.do(lambda e: e.reciprocal(nrm[:, c:c + m], nrm[:, c:c + m]), s_node)
                dve.wait(s_node, n)
                dve.wait(s_node, x_ready[c])
                for j in range(m):
                    n = dve.do(lambda e, j=j: e.scalar_tensor_tensor(
                        out=x[:, c + j, :], in0=o[:, j, :], scalar=nrm[:, c + j:c + j + 1], in1=x[:, c + j, :],
                        op0=ALU.mult, op1=ALU.add), s_node)
                x_ready[c] = n
                node_free["tmp%d" % slot] = [(s_node, n)]
            else:
                n = xadd(c, m, lambda e: e.tensor_tensor(out=xc, in0=v, in1=xc, op=ALU.add))
                node_free[key] = [(s_node, n)]
                sp.wait(s_node, n)
                last = c + m == nb
                full = m - 1 if last else m
                if full:
                    sp.dma(lambda e: e.dma_start(out[c * P:(c + full) * P, :].rearrange("(b p) f -> p b f", p=P),
                                                 x[:, c:c + full, :]), s_out)
                if last:
                    sp.dma(lambda e: e.dma_start(out[(nb - 1) * P:n_nodes, :], x[0:last_rows, nb - 1, :]), s_out)

        slot_free = {}

        def edges(layer):
            table, idx = {0: (tab_h[0], idx_src), 1: (tab_h[1], idx_src),
                          2: (tab_m, idx_src), 3: (tab_rel, idx_rel)}[layer]
            for s, v in tab_done.items():
                pool.wait(s, v)
                if layer == 1:
                    sp.wait(s, v)
            tab_done.clear()
            tiles = [min(TPG, nt - g * TPG) for g in range(ng)]
            a_free = {}
            n_row, n_one, n_scat, n_bc, n_pw, n_oneT, n_gT, n_exp, n_act, n_z, n_gate = ({} for _ in range(11))
            sums = 2 if layer < 2 else 1

            def gather(g):
                sl = g % NSLOT
                for s, v in slot_free.get(sl, ()):
                    pool.wait(s, v)
                for t in range(tiles[g]):
                    col = g * TPG + t
                    n_row[g] = pool.dma(lambda e, t=t, col=col: e.indirect_dma_start(
                        out=rows[:, sl, t, :], out_offset=None, in_=table[:, :],
                        in_offset=bass.IndirectOffsetOnAxis(ap=idx[:, col:col + 1], axis=0)), s_row[sl])

            def onehot(g):
                sl, m = g % NONE, tiles[g]
                o = oneh[:, sl, 0:m, :]
                rel = dst_rel[:, g * TPG:g * TPG + m].unsqueeze(2).to_broadcast([P, m, WIN])
                if g >= NONE:
                    dve.wait(s_scat, n_scat[g - NONE])
                n = dve.do(lambda e: e.tensor_tensor(out=o, in0=iota_w.unsqueeze(1).to_broadcast([P, m, WIN]),
                                                     in1=rel, op=ALU.is_equal), s_one)
                if layer == 3:
                    dve.wait(s_one, n)
                    n = dve.do(lambda e: e.tensor_tensor(
                        out=o, in0=o, in1=wt[:, g * TPG:g * TPG + m].unsqueeze(2).to_broadcast([P, m, WIN]), op=ALU.mult), s_one)
                n_one[g] = n

            def scatter(g):
                sl, m = g % NONE, tiles[g]
                bank = ps_a[g % 2]
                pe.wait(s_one, n_one[g])
                pe.wait(s_row[g % NSLOT], n_row[g])
                pe.wait(s_add, a_free.get(g % 2, 0))
                for t in range(m):
                    f = lambda e, t=t: e.matmul(bank[:, 0:WIN], rows[:, g % NSLOT, t, :], oneh[:, sl, t, :],
                                                start=t == 0, stop=t == m - 1)
                    last = sums == 1 and t == m - 1
                    n = pe.do(f, s_scat) if last else pe.do(f)
                if sums == 2:
                    for t in range(m):
                        f = lambda e, t=t: e.matmul(bank[:, WIN:2 * WIN], ones[:, :], oneh[:, sl, t, :],
                                                    start=t == 0, stop=t == m - 1)
                        n = pe.do(f, s_scat) if t == m - 1 else pe.do(f)
                n_scat[g] = n
                slot_free[g % NSLOT] = [(s_scat, n)]

            def accumulate(g):
                dve.wait(s_scat, n_scat[g])
                if s_add.value:
                    dve.wait(s_add, s_add.value)

                def make(e):
                    start = e.value_load(base_int[0:1, g:g + 1], min_val=0, max_val=npad - WIN)
                    a = acc[:, 0:sums, bass.ds(start, WIN)]
                    v = ps_a[g % 2][:, 0:sums * WIN].rearrange("p (k w) -> p k w", k=sums)
                    return e.tensor_tensor(out=a, in0=a, in1=v, op=ALU.add)
                a_free[g % 2] = dve.do(make, s_add)

            def fetch_window(g):
                sl, m = g % 3, tiles[g]
                if g >= 3:
                    sp.wait(s_oneT, n_oneT[g - 3])
                    sp.wait(s_hid, n_exp[g - 3])
                n_bc[g] = sp.dma(lambda e: e.dma_start(
                    dst_bc[:, sl, 0:m * P], dst_flat[g * TPG * P:(g * TPG + m) * P].partition_broadcast(WIN)), s_bc[sl])

                def make(e):
                    start = e.value_load(base_int[0:1, g:g + 1], min_val=0, max_val=npad - WIN)
                    return e.dma_start(pwin[:, sl, :], tab_p[bass.ds(start, WIN), :])
                n_pw[g] = sp.dma(make, s_pw[sl])

            def onehot_t(g):
                m = tiles[g]
                dve.wait(s_bc[g % 3], n_bc[g])
                if g >= 2:
                    dve.wait(s_hid, n_exp[g - 2])
                n_oneT[g] = dve.do(lambda e: e.tensor_scalar(
                    onehT[:, g % 2, 0:m * P], dst_bc[:, g % 3, 0:m * P], win_node[0:WIN, g:g + 1], None, ALU.is_equal), s_oneT)

            def turn_rows(g):
                m, sl = tiles[g], g % 2
                pe.wait(s_row[g % NSLOT], n_row[g])
                if g >= 2:
                    pe.wait(s_gT, n_gT[g - 2])
                for t in range(m):
                    f = lambda e, t=t: e.transpose(ps_t[sl][:, t * P:(t + 1) * P], rows[:, g % NSLOT, t, :], ident[:, :])
                    n = pe.do(f, s_rowT) if t == m - 1 else pe.do(f)
                act.wait(s_rowT, n)
                if g >= 2:
                    act.wait(s_hid, n_exp[g - 2])
                n_gT[g] = act.do(lambda e: e.copy(hT[:, sl, 0:m * P], ps_t[sl][:, 0:m * P]), s_gT)

            def hidden(g):
                m, sl = tiles[g], g % 2
                v = ps_e[sl][:, 0:m * P]
                pe.wait(s_oneT, n_oneT[g])
                pe.wait(s_pw[g % 3], n_pw[g])
                if g >= 2:
                    pe.wait(s_act, n_act[g - 2])
                pe.do(lambda e: e.matmul(v, pwin[:, g % 3, :], onehT[:, sl, 0:m * P], start=True, stop=False))
                pe.wait(s_gT, n_gT[g])
                n_exp[g] = pe.do(lambda e: e.matmul(v, w1neg[:, :], hT[:, sl, 0:m * P], start=False, stop=True), s_hid)
                act.wait(s_hid, n_exp[g])
                if g >= 2:
                    act.wait(s_z, n_z[g - 2])
                n_act[g] = act.do(lambda e: e.activation(hid[:, sl, 0:m * P], v, ACT.Relu, bias=b1col[:, 0:1]), s_act)

            def gates(g):
                m, sl = tiles[g], g % 2
                pe.wait(s_act, n_act[g])
                if g >= 2:
                    pe.wait(s_gate, n_gate[g - 2])
                for t in range(m):
                    f = lambda e, t=t: e.matmul(ps_m[sl][:, t:t + 1], hid[:, sl, t * P:(t + 1) * P], w2col[:, :], start=True, stop=True)
                    n = pe.do(f, s_z) if t == m - 1 else pe.do(f)
                n_z[g] = n
                act.wait(s_z, n)
                if g >= 2:
                    act.wait(s_one, n_one2[g - 2])
                n_gate[g] = act.do(lambda e: e.activation(gate[:, sl, 0:m], ps_m[sl][:, 0:m], ACT.Sigmoid, bias=b2[:, 0:1]), s_gate)

            n_one2 = {}

            def weigh(g):
                m, sl = tiles[g], g % NONE
                dve.wait(s_gate, n_gate[g])
                dve.wait(s_one, n_one[g])
                o = oneh[:, sl, 0:m, :]
                n_one[g] = dve.do(lambda e: e.tensor_tensor(
                    out=o, in0=o, in1=gate[:, g % 2, 0:m].unsqueeze(2).to_broadcast([P, m, WIN]), op=ALU.mult), s_one)
                n_one2[g] = n_one[g]

            dve.wait(s_zero, s_zero.value)
            if layer != 1:
                for g in range(ng):
                    gather(g)
                    onehot(g)
                    scatter(g)
                    if g >= 1:
                        accumulate(g - 1)
                accumulate(ng - 1)
            else:
                steps = ((4, accumulate), (3, weigh), (3, scatter), (2, gates), (1, hidden),
                         (0, gather), (0, fetch_window), (0, turn_rows), (0, onehot_t), (2, onehot))
                for turn in range(ng + 4):
                    for behind, step in steps:
                        if 0 <= turn - behind < ng:
                            step(turn - behind)
            general(layer, table, idx, sums)

        def general(layer, table, idx, sums):
            q = gen_sems[layer]
            rowbuf = rows[:, 0, :, :]
            one = rows[:, 1, :, :]
            p_dst = rows[:, 2, :, :]
            p_src = rows[:, 3, :, :]
            bank = ps_a[0]

            def guarded(body):
                def run(eng):
                    flag = eng.value_load(outside[0:1, 0:1], min_val=0, max_val=n_edges)
                    with eng.If(flag):
                        body(eng)
                return run

            def on_dve(e):
                with e.Fori(0, ng) as g:
                    cols = bass.ds(g * TPG, TPG)
                    rel = dst_rel[:, cols]
                    e.tensor_copy(gen_idx[:, :], idx[:, cols])
                    if layer == 3:
                        e.tensor_copy(gen_wt[:, :], wt[:, cols])
                    e.tensor_scalar(gen_in[:, :], rel, 0.0, None, ALU.is_ge)
                    e.tensor_scalar(gen_abs[:, :], rel, win_node[:, bass.ds(g, 1)], None, ALU.add)
                    e.drain()
                    e.scalar_tensor_tensor(out=gen_in[:, :], in0=rel, scalar=float(WIN), in1=gen_in[:, :],
                                           op0=ALU.is_lt, op1=ALU.mult)
                    e.tensor_scalar(gen_abs[:, :], gen_abs[:, :], iota_p[:, 0:1], None, ALU.subtract)
                    e.drain()
                    e.scalar_tensor_tensor(out=gen_dst[:, :], in0=gen_in[:, :], scalar=-4.0 * npad, in1=gen_abs[:, :],
                                           op0=ALU.mult, op1=ALU.add)
                    e.tensor_scalar(gen_tgt[:, :], gen_abs[:, :], 0.0, None, ALU.max)
                    e.drain().then_inc(q["idx"], 1)
                    if layer == 1:
                        e.wait_ge(q["prow"], (g + 1) * (2 * 16 * TPG))
                        dd = p_dst
                        e.tensor_tensor(out=dd, in0=p_dst, in1=p_src, op=ALU.subtract)
                        e.drain()
                        e.tensor_tensor(out=dd, in0=dd, in1=bcast(bias1, TPG), op=ALU.add)
                        e.drain()
                        e.scalar_tensor_tensor(out=dd, in0=dd, scalar=0.0, in1=bcast(w2, TPG), op0=ALU.max, op1=ALU.mult)
                        e.drain()
                        e.tensor_reduce(out=zed[:, :], in_=dd, axis=AXX, op=ALU.add).then_inc(q["z"], 1)
                        e.wait_ge(q["gate"], g + 1)
                        e.tensor_copy(gen_wt[:, :], gate[:, 0, :])
                        e.drain()
                    with e.Fori(0, nb) as b:
                        done = g * nb + b
                        e.tensor_tensor(out=one, in0=iota_b[:, :].unsqueeze(1).to_broadcast([P, TPG, P]),
                                        in1=gen_dst[:, :].unsqueeze(2).to_broadcast([P, TPG, P]), op=ALU.is_equal)
                        e.drain()
                        e.tensor_scalar(gen_dst[:, :], gen_dst[:, :], float(P), None, ALU.subtract)
                        if layer in (1, 3):
                            e.tensor_tensor(out=one, in0=one, in1=gen_wt[:, :].unsqueeze(2).to_broadcast([P, TPG, P]),
                                            op=ALU.mult)
                        e.drain().then_inc(q["one"], 1)
                        e.wait_ge(q["scat"], done + 1)
                        a = acc[:, 0:sums, bass.ds(b * P, P)]
                        v = bank[:, 0:sums * P].rearrange("p (k w) -> p k w", k=sums)
                        e.tensor_tensor(out=a, in0=a, in1=v, op=ALU.add)
                        e.drain()

            def on_pool(e):
                with e.Fori(0, ng) as g:
                    e.wait_ge(q["idx"], g + 1)
                    e.sem_inc(q["seen"])
                    for t in range(TPG):
                        e.indirect_dma_start(out=rowbuf[:, t, :], out_offset=None, in_=table[:, :],
                                             in_offset=bass.IndirectOffsetOnAxis(ap=gen_idx[:, t:t + 1], axis=0)
                                             ).then_inc(q["row"], 16)
                    for buf, num in ((p_dst, gen_tgt), (p_src, gen_idx)) if layer == 1 else ():
                        for t in range(TPG):
                            e.indirect_dma_start(out=buf[:, t, :], out_offset=None, in_=tab_p[:, :],
                                                 in_offset=bass.IndirectOffsetOnAxis(ap=num[:, t:t + 1], axis=0)
                                                 ).then_inc(q["prow"], 16)

            def on_act(e):
                with e.Fori(0, ng) as g:
                    e.wait_ge(q["z"], g + 1)
                    e.activation(gate[:, 0, :], zed[:, :], ACT.Sigmoid, bias=b2[:, 0:1]).then_inc(q["gate"], 1)

            def on_pe(e):
                with e.Fori(0, ng) as g:
                    e.wait_ge(q["row"], (g + 1) * (16 * TPG))
                    e.sem_inc(q["seen"])
                    with e.Fori(0, nb) as b:
                        e.wait_ge(q["one"], g * nb + b + 1)
                        for t in range(TPG):
                            last = e.matmul(bank[:, 0:P], rowbuf[:, t, :], one[:, t, :], start=t == 0, stop=t == TPG - 1)
                        for t in range(TPG if sums == 2 else 0):
                            last = e.matmul(bank[:, P:2 * P], ones[:, :], one[:, t, :], start=t == 0, stop=t == TPG - 1)
                        last.then_inc(q["scat"], 1)

            dve.wait(s_add, s_add.value)
            dve.do(guarded(on_dve))
            pool.do(guarded(on_pool))
            pe.do(guarded(on_pe))
            if layer == 1:
                act.do(guarded(on_act))
            dve.do(lambda e: e.drain(), s_gen)

        def ones_sums(keep):
            pe.wait(s_gen, s_gen.value)
            wait_free(pe, "ps_t0")
            for b in range(nb):
                f = lambda e, b=b: e.matmul(ps_t[0][:, b:b + 1], acc[0:1, 1, b * P:(b + 1) * P], ones[0:1, 0:1], start=True, stop=True)
                n = pe.do(f, s_cnt) if b == nb - 1 else pe.do(f)
            dve.wait(s_cnt, n)
            if keep == "degree":
                n = dve.do(lambda e: e.tensor_copy(indeg[:, :], ps_t[0][:, 0:nb]), s_node)
                dve.wait(s_node, n)
                n = dve.do(lambda e: e.tensor_scalar(rdeg[:, :], indeg[:, :], 1.0, None, ALU.max), s_node)
                dve.wait(s_node, n)
                n = dve.do(lambda e: e.reciprocal(rdeg[:, :], rdeg[:, :]), s_node)
            else:
                n = dve.do(lambda e: e.tensor_copy(sumw[:, :], ps_t[0][:, 0:nb]), s_node)
            dve.wait(s_node, n)
            node_free["ps_t0"] = [(s_node, n)]

        def node_chunk(layer, i, c, m):
            yield from node_post(layer, i, c, m, [(s_add, s_add.value), (s_gen, s_gen.value)])
            if layer < 3:
                yield
                yield from node_pre(layer + 1, i, c, m)

        def interleave(chains):
            chains, running = list(chains), []
            while chains or running:
                if chains:
                    running.append(chains.pop(0))
                running = [r for r in running if next(r, "end") != "end"]

        interleave(node_pre(0, i, c, m) for i, (c, m) in enumerate(chunks))
        dve.wait(s_win, n_win)
        dve.do(lambda e: e.tensor_copy(f_src, raw_src), s_prep)
        n_dst = dve.do(lambda e: e.tensor_copy(f_dst, raw_dst), s_prep)
        n = dve.do(lambda e: e.tensor_copy(f_rel, raw_typ), s_prep)
        dve.wait(s_prep, n)
        n_flt = dve.do(lambda e: e.scalar_tensor_tensor(out=f_rel, in0=f_src, scalar=float(n_rel), in1=f_rel,
                                                op0=ALU.mult, op1=ALU.add), s_prep)
        sp.wait(s_prep, n_dst)
        n_dstf = sp.dma(lambda e: e.dma_start(dst_flat.rearrange("(b p e) -> p b e", p=P, e=P),
                                     f_dst.rearrange("p (b e) -> p b e", e=P)), s_dstf)

        pe.wait(s_prep, n_flt)
        wait_free(pe, "ps_t0")
        wait_free(pe, "ps_t1")
        bank_free = {}
        k = 0
        for srcv, dstv in ((f_dst, dst_rel), (f_src, idx_src), (f_rel, idx_rel), (raw_wt, wt)):
            for b0 in range(0, nr, CH):
                m = min(CH, nr - b0)
                bank = ps_t[k % 2]
                pe.wait(s_prep, bank_free.get(k % 2, 0))
                for j in range(m):
                    blk = srcv[:, (b0 + j) * P:(b0 + j + 1) * P]
                    ins_ = (lambda e, bank=bank, j=j, blk=blk: e.transpose(bank[:, j * P:(j + 1) * P], blk, ident[:, :]))
                    n = pe.do(ins_, s_prepT) if j == m - 1 else pe.do(ins_)
                dve.wait(s_prepT, n)
                bank_free[k % 2] = dve.do(lambda e, bank=bank, b0=b0, m=m, dstv=dstv: e.tensor_copy(
                    dstv[:, b0 * P:(b0 + m) * P], bank[:, 0:m * P]), s_prep)
                k += 1
        n_tab = s_prep.value
        dve.wait(s_prep, n_tab)
        first = dst_rel[0:1, 0:ng * TPG].rearrange("p (g t) -> p g t", t=TPG)[:, :, 0]
        dve.do(lambda e: e.tensor_scalar(base_row[:, :], first, float(npad - WIN), None, ALU.min), s_prep)
        dve.wait(s_prep, s_prep.value)
        n_base = dve.do(lambda e: e.tensor_copy(base_int[:, :], base_row[:, :]), s_prep)
        pe.wait(s_prep, n_base)
        n = pe.do(lambda e: e.matmul(ps_t[0][:, 0:ng], ones[0:1, :], base_row[:, :], start=True, stop=True), s_prepT)
        dve.wait(s_prepT, n)
        gd = dst_rel[:, 0:ng * TPG].rearrange("p (g t) -> p g t", t=TPG)
        n = dve.do(lambda e: e.tensor_tensor(out=gd, in0=gd, in1=ps_t[0][:, 0:ng].unsqueeze(2).to_broadcast([P, ng, TPG]),
                                         op=ALU.subtract), s_prep)
        n_prep = dve.do(lambda e: e.tensor_scalar(win_node[:, :], ps_t[0][:, 0:ng], iota_p[:, 0:1], None, ALU.add), s_prep)

        gi = f_rel[:, 0:ng * TPG].rearrange("p (g t) -> p g t", t=TPG)
        dve.wait(s_prep, n_prep)
        n = dve.do(lambda e: e.tensor_scalar(gi, gd, 0.0, None, ALU.is_ge), s_prep)
        dve.wait(s_prep, n)
        n = dve.do(lambda e: e.scalar_tensor_tensor(out=gi, in0=gd, scalar=float(WIN), in1=gi, op0=ALU.is_lt, op1=ALU.mult), s_prep)
        dve.wait(s_prep, n)
        n = dve.do(lambda e: e.tensor_reduce(out=n_inside[:, :], in_=f_rel[:, 0:ng * TPG], axis=AXX, op=ALU.add), s_prep)
        pe.wait(s_prep, n)
        n = pe.do(lambda e: e.matmul(ps_t[0][:, 0:1], ones[:, :], n_inside[:, :], start=True, stop=True), s_prepT)
        dve.wait(s_prepT, n)
        dve.do(lambda e: e.tensor_scalar(outside[:, :], ps_t[0][0:1, 0:1], -1.0, float(n_edges), ALU.mult, ALU.add), s_prep)

        n_prep = s_prep.value
        dve.wait(s_prep, n_prep)
        for q in (pe, pool, sp):
            q.wait(s_prep, n_prep)
        for q in (pool, sp):
            q.wait(s_dstf, n_dstf)
        n_zero = pool.do(lambda e: e.memset(acc[:, :, :], 0.0), s_zero)
        node_free["ps_t0"] = node_free["ps_t1"] = [(s_prep, n_prep)]
        for layer in range(4):
            edges(layer)
            if layer < 2:
                ones_sums(("degree", "gates")[layer])
                node_free["sums_read"] = [(s_cnt, s_cnt.value)]
            interleave(node_chunk(layer, i, c, m) for i, (c, m) in enumerate(chunks))
        sp.wait(s_out, s_out.value)

        block = ctx.enter_context(nc.Block())
        block.sync(lambda eng: sp.emit(eng))
        block.gpsimd(lambda eng: pool.emit(eng))
        block.scalar(lambda eng: act.emit(eng))
        block.vector(lambda eng: dve.emit(eng))
        block.tensor(lambda eng: pe.emit(eng))


_INS = ["x", "src", "dst", "edge_type_8", "edge_weight1", "L0_gnn_W", "L0_gnn_b", "L1_gnn_W1", "L1_gnn_b1",
        "L1_gnn_W2", "L1_gnn_b2", "L1_gnn_W4", "L1_gnn_b4", "L2_gnn_Wp", "L2_gnn_bp", "L2_gnn_Wl", "L2_gnn_bl",
        "L2_gnn_Wr", "L3_gnn_weight", "L3_gnn_loop_weight"]


def kernel(**inputs):
    import numpy as np
    import concourse.bacc as bacc
    from concourse.bass_utils import run_bass_kernel_spmd

    nc = bacc.Bacc("TRN2", target_bir_lowering=False, num_devices=1)
    arrays, args = {}, {}
    for name in _INS:
        a = np.ascontiguousarray(inputs[name])
        arrays["in_" + name] = a
        args[name] = nc.dram_tensor("in_" + name, a.shape, mybir.dt.from_np(a.dtype), kind="ExternalInput").ap()
    out = nc.dram_tensor("out_x", args["x"].shape, F32, kind="ExternalOutput").ap()
    gnn_program(nc, args, out)
    r = run_bass_kernel_spmd(nc, [arrays], core_ids=[0])
    return r.results[0]["out_x"]
```

```python
import concourse.bass as bass
from concourse import mybir
from concourse.alu_op_type import AluOpType as ALU
from contextlib import ExitStack

ACT = mybir.ActivationFunctionType
AXX = mybir.AxisListType.X
F32, I32, U32, BF16 = mybir.dt.float32, mybir.dt.int32, mybir.dt.uint32, mybir.dt.bfloat16

P = 128
TPG = 4
WIN = 64
CH = 4
NSLOT = 10
NONE = 3
PACKS = ((16, 160 / 1563, 16), (16, 160 / 1563, 32), (8, 192 / 1563, 32))
BUNDLE = 64
ACT_TILES = (2, 5, 7)
NORM_BATCH = 3
STEPS_TO_H = 3
PACK_LEAD = 1.08
NQS = 3
EPS_LN, EPS_NORM = 1e-5, 1e-12


class Sem:

    def __init__(self, handle):
        self.handle, self.value = handle, 0


class Queue:

    def __init__(self):
        self.items = []

    def do(self, make, sem=None, by=1):
        if sem is None:
            self.items.append(lambda eng: make(eng))
            return None
        sem.value += by
        self.items.append(lambda eng: make(eng).then_inc(sem.handle, by))
        return sem.value

    def dma(self, make, sem):
        return self.do(make, sem, 16)

    def wait(self, sem, value):
        if value:
            self.items.append(lambda eng: eng.wait_ge(sem.handle, value))

    def emit(self, eng):
        for item in self.items:
            item(eng)


def gnn_program(nc, ins, out):
    x_in = ins["x"]
    n_nodes, d = x_in.shape
    n_edges = ins["src"].shape[0]
    n_rel = ins["L3_gnn_weight"].shape[0]
    assert d == P
    nb = -(-n_nodes // P)
    npad = nb * P
    nt = -(-n_edges // P)
    ng = -(-nt // TPG)
    nr = -(-nt // P)
    packs = []
    bundles = []
    sections = []
    first = 0
    for size, share, window in PACKS:
        count = int(share * nt / size + 1e-6)
        sections.append((first, size, count, window))
        packs += [(first + k * size, size, window) for k in range(count)]
        for k in range(len(packs) - count, len(packs), BUNDLE // window):
            bundles.append(list(range(k, min(k + BUNDLE // window, len(packs)))))
        first += count * size
    npt = first
    npg = npt // TPG
    chunks = [(c, min(CH, nb - c)) for c in range(0, nb, CH)]
    full_tiles = n_edges // P
    rest_edges = n_edges - full_tiles * P
    last_rows = n_nodes - (nb - 1) * P

    with ExitStack() as ctx:
        def sb(name, shape, dt=F32):
            return ctx.enter_context(nc.sbuf_tensor(name, shape, dt))

        def sem(name):
            return Sem(ctx.enter_context(nc.semaphore(name)))

        def dram(name, shape, dt=F32):
            return nc.dram_tensor(name, shape, dt, kind="Internal").ap()

        tab_h = [dram(f"tab_h{i}", (npad, P)) for i in range(2)]
        tab_p = dram("tab_p", (npad, P))
        tab_m = dram("tab_m", (npad, P))
        tab_rel = dram("tab_rel", (npad * n_rel, P))
        dst_flat = dram("dst_flat", (nr * P * P,))

        x = sb("x", [P, nb, P])
        h = sb("h", [P, nb, P])
        acc = sb("acc", [P, 2, npad])
        rself = acc[:, 1, :].rearrange("p (b f) -> p b f", f=P)
        rows = sb("rows", [P, NSLOT, TPG, P])
        spare = rows[:, :, :, :].rearrange("p a b c -> p (a b c)")
        stage = spare[:, 0:2 * CH * P].rearrange("p (s b f) -> p s b f", s=2, f=P)
        stage2 = spare[:, 2 * CH * P:4 * CH * P].rearrange("p (s b f) -> p s b f", s=2, f=P)
        stage_rel = spare[:, 0:3 * n_rel * P].rearrange("p (s f) -> p s f", s=3)
        raw = acc[:, :, :].rearrange("p k n -> p (k n)")
        idx_src = sb("idx_src", [P, nr * P], U32)
        idx_rel = sb("idx_rel", [P, nr * P], U32)
        dst_rel = sb("dst_rel", [P, nr * P])
        wt = sb("wt", [P, nr * P])
        win_node = sb("win_node", [P, ng])
        base_row = sb("base_row", [1, ng])
        base_int = sb("base_int", [1, ng], I32)
        n_key = nb * max(w for _, _, _, w in sections)
        n_counts = nb * BUNDLE + NQS * n_key // 2
        cut = [0]
        for words in (3 * TPG * P, 2 * TPG * P, 3 * P, 2 * TPG * P):
            cut.append(cut[-1] + words)
        shared = sb("shared", [P, max(n_counts + TPG * P, cut[-1])])
        counts = shared[:, 0:nb * BUNDLE].rearrange("p (q w) -> p q w", w=BUNDLE)
        pairs = shared[:, nb * BUNDLE:n_counts].bitcast(BF16).rearrange("p (s k) -> p s k", s=NQS)
        srow = shared[:, n_counts:n_counts + TPG * P].bitcast(BF16)
        srow = srow.rearrange("p (s t r) -> p s t r", s=2, r=P)
        dst_bc = shared[0:WIN, cut[0]:cut[1]].rearrange("p (s e) -> p s e", s=3)
        onehT = shared[0:WIN, cut[1]:cut[2]].rearrange("p (s e) -> p s e", s=2)
        pwin = shared[0:WIN, cut[2]:cut[3]].rearrange("p (s f) -> p s f", s=3)
        hid = shared[:, cut[3]:cut[4]].rearrange("p (s e) -> p s e", s=2)
        tmp = shared[:, 0:4 * CH * P].rearrange("p (s b f) -> p s b f", s=4, f=P)
        key = sb("key", [P, npt])
        src_row = sb("src_row", [P, npt])
        iota_k = sb("iota_k", [P, n_key], mybir.dt.int16)
        csum = sb("csum", [P, BUNDLE])
        wsum = sb("wsum", [BUNDLE, P])
        oneh = sb("oneh", [P, NONE, TPG, WIN])
        onesumb = sb("onesumb", [P, 2, WIN], BF16)
        onesb = sb("onesb", [P, P], BF16)
        onesum = sb("onesum", [P, 2, WIN])
        zed = sb("zed", [P, TPG])
        b1col = sb("b1col", [P, 1])
        w2col = sb("w2col", [P, 1])
        w1neg = sb("w1neg", [P, P])
        nmr = sb("nmr", [P, nb])
        gate = sb("gate", [P, 2, TPG])
        hT = sb("hT", [P, 2, CH * P])
        stats = sb("stats", [P, nb, 6])
        mv = sb("mv", [P, nb, 2])
        std = sb("std", [P, nb])
        rstd = sb("rstd", [P, nb])
        indeg = sb("indeg", [P, nb])
        rdeg = sb("rdeg", [P, nb])
        sumw = sb("sumw", [P, nb])
        nrm = sb("nrm", [P, nb])
        ident = sb("ident", [P, P])
        ones = sb("ones", [P, P])
        iota_b = sb("iota_b", [P, P])
        iota_w = iota_b[:, 0:WIN]
        iota_p = sb("iota_p", [P, 1])
        eps_ln = sb("eps_ln", [P, 1])
        b2 = sb("b2", [P, 1])
        w0 = sb("w0", [P, 2 * P])
        w0a, w0b = sb("w0a", [P, P]), sb("w0b", [P, P])
        w1, w4 = sb("w1", [P, P]), sb("w4", [P, P])
        wp, wl, wr = sb("wp", [P, P]), sb("wl", [P, P]), sb("wr", [P, P])
        wpT, wlT, wrT = sb("wpT", [P, P]), sb("wlT", [P, P]), sb("wrT", [P, P])
        wrel = sb("wrel", [P, n_rel * P])
        wloop = sb("wloop", [P, P])
        bias0, bias1, bias4, biasp, biasl, w2 = (sb(n, [P, P]) for n in ("bias0", "bias1", "bias4", "biasp", "biasl", "w2"))
        n_inside = sb("n_inside", [P, 1])
        outside = sb("outside", [1, 1], I32)
        gen_idx = sb("gen_idx", [P, TPG], U32)
        gen_tgt = sb("gen_tgt", [P, TPG], U32)
        gen_dst = sb("gen_dst", [P, TPG])
        gen_abs = sb("gen_abs", [P, TPG])
        gen_in = sb("gen_in", [P, TPG])
        gen_wt = sb("gen_wt", [P, TPG])

        ps = [ctx.enter_context(nc.psum_tensor(f"ps{i}", [P, 512], F32)) for i in range(8)]
        ps_t, ps_m, ps_e, ps_a = ps[0:2], ps[2:4], ps[4:6], ps[6:8]

        s_const = sem("s_const")
        s_win = sem("s_win")
        s_wgt = sem("s_wgt")
        s_xin = [sem(f"s_xin{i}") for i in range(len(chunks))]
        s_pad = sem("s_pad")
        s_prep = sem("s_prep")
        s_prepT = sem("s_prepT")
        s_dstf = sem("s_dstf")
        s_ln = sem("s_ln")
        s_sqrt = sem("s_sqrt")
        s_h = sem("s_h")
        s_tr = sem("s_tr")
        s_hT = sem("s_hT")
        s_mm = sem("s_mm")
        s_node = sem("s_node")
        s_relu = sem("s_relu")
        s_tab = [sem(f"s_tab{i}") for i in range(3)]
        s_tabh = sem("s_tabh")
        s_zero = sem("s_zero")
        s_row = [sem(f"s_row{i}") for i in range(NSLOT)]
        s_one = sem("s_one")
        s_osum = sem("s_osum")
        s_scat = sem("s_scat")
        s_add = sem("s_add")
        s_bc = [sem(f"s_bc{i}") for i in range(3)]
        s_pw = [sem(f"s_pw{i}") for i in range(3)]
        s_oneT = sem("s_oneT")
        s_rowT = sem("s_rowT")
        s_gT = sem("s_gT")
        s_hid = sem("s_hid")
        s_act = sem("s_act")
        s_z = sem("s_z")
        s_gate = sem("s_gate")
        s_cnt = sem("s_cnt")
        s_out = sem("s_out")
        s_pair = sem("s_pair")
        s_paira = sem("s_paira")
        s_srow = sem("s_srow")
        s_count = sem("s_count")
        s_cev = sem("s_cev")
        s_csum = sem("s_csum")
        s_pack = sem("s_pack")
        s_wev = sem("s_wev")
        s_turn = sem("s_turn")
        s_gen = sem("s_gen")
        gen_sems = [{k: ctx.enter_context(nc.semaphore(f"g{layer}_{k}")) for k in
                     ("idx", "row", "prow", "z", "gate", "one", "scat", "seen")} for layer in range(4)]

        pe, dve, act, pool, sp = (Queue() for _ in range(5))

        pool.do(lambda e: e.memset(ident[:, :], 0.0), s_const)
        pool.do(lambda e: e.memset(ones[:, :], 1.0), s_const)
        pool.do(lambda e: e.memset(onesb[:, :], 1.0), s_const)
        pool.do(lambda e: e.memset(eps_ln[:, :], EPS_LN), s_const)
        pool.do(lambda e: e.iota(iota_b[:, :], [[1, P]], base=0, channel_multiplier=0,
                                 allow_small_or_imprecise_dtypes=True), s_const)
        n = pool.do(lambda e: e.iota(iota_p[:, :], [[1, 1]], base=0, channel_multiplier=1,
                                     allow_small_or_imprecise_dtypes=True), s_const)
        n = pool.do(lambda e: e.iota(iota_k[:, :], [[1, n_key]], base=0, channel_multiplier=0), s_const)
        pool.wait(s_const, n)
        n_const = pool.do(lambda e: e.affine_select(
            out=ident[:, :], in_=ident[:, :], compare_op=ALU.not_equal, fill=1.0,
            base=0, pattern=[[-1, P]], channel_multiplier=1), s_const)

        rblk = nr * P
        raw_src = raw[:, 0 * rblk:1 * rblk].bitcast(I32)
        raw_dst = raw[:, 1 * rblk:2 * rblk].bitcast(I32)
        raw_typ = raw[:, 2 * rblk:3 * rblk].bitcast(I32)
        raw_wt = raw[:, 3 * rblk:4 * rblk]
        f_src, f_dst, f_rel = (spare[:, i * rblk:(i + 1) * rblk] for i in range(3))
        assert 4 * rblk <= 2 * npad and 3 * rblk <= NSLOT * TPG * P
        body = (nr - 1) * P
        tail = full_tiles - body
        pads = ((raw_src, 0), (raw_dst, -1), (raw_typ, 0), (raw_wt, 0))
        dve.do(lambda e: e.memset(x[:, nb - 1, :], 0.0), s_pad)
        for v, fill in pads:
            n_pad = dve.do(lambda e, v=v, fill=fill: e.memset(v[:, body:rblk], fill), s_pad)
        sp.wait(s_pad, n_pad)
        for i, (c, m) in enumerate(chunks):
            full = m - 1 if c + m == nb else m
            if full:
                sp.dma(lambda e, c=c, full=full: e.dma_start(
                    x[:, c:c + full, :], x_in[c * P:(c + full) * P, :].rearrange("(b p) f -> p b f", p=P)), s_xin[i])
            if c + m == nb:
                sp.dma(lambda e: e.dma_start(x[0:last_rows, nb - 1, :], x_in[(nb - 1) * P:n_nodes, :]), s_xin[i])
        for name, v in (("src", raw_src), ("dst", raw_dst), ("edge_type_8", raw_typ), ("edge_weight1", raw_wt)):
            a = ins[name]
            if len(a.shape) == 2:
                a = a.rearrange("n o -> (n o)")
            v3 = v.rearrange("p (b e) -> p b e", e=P)
            sp.dma(lambda e, a=a, v3=v3: e.dma_start(
                v3[:, 0:nr - 1, :], a[0:body * P].rearrange("(b p e) -> p b e", p=P, e=P)), s_win)
            sp.dma(lambda e, a=a, v3=v3: e.dma_start(
                v3[0:tail, nr - 1, :], a[body * P:full_tiles * P].rearrange("(p e) -> p e", e=P)), s_win)
            if rest_edges:
                n_win = sp.dma(lambda e, a=a, v3=v3: e.dma_start(
                    v3[tail:tail + 1, nr - 1, 0:rest_edges],
                    a[full_tiles * P:n_edges].rearrange("(p e) -> p e", p=1)), s_win)
        n_win = s_win.value
        for t, a in ((w0, ins["L0_gnn_W"]), (w1, ins["L1_gnn_W1"]), (w4, ins["L1_gnn_W4"]), (wp, ins["L2_gnn_Wp"]),
                     (wl, ins["L2_gnn_Wl"]), (wr, ins["L2_gnn_Wr"]), (wloop, ins["L3_gnn_loop_weight"])):
            act.dma(lambda e, t=t, a=a: e.dma_start(t[:, :], a), s_wgt)
        act.dma(lambda e: e.dma_start(wrel[:, :].rearrange("p (r o) -> p r o", r=n_rel),
                                      ins["L3_gnn_weight"].rearrange("r i o -> i r o")), s_wgt)
        for t, a in ((bias0, ins["L0_gnn_b"]), (bias1, ins["L1_gnn_b1"]), (bias4, ins["L1_gnn_b4"]),
                     (biasp, ins["L2_gnn_bp"]), (biasl, ins["L2_gnn_bl"]),
                     (w2, ins["L1_gnn_W2"].rearrange("n o -> (n o)")), (b2, ins["L1_gnn_b2"])):
            act.dma(lambda e, t=t, a=a: e.dma_start(t[:, :], a.partition_broadcast(P)), s_wgt)
        act.dma(lambda e: e.dma_start(b1col[:, :], ins["L1_gnn_b1"].rearrange("(p o) -> p o", o=1)), s_wgt)
        act.dma(lambda e: e.dma_start(w2col[:, :], ins["L1_gnn_W2"]), s_wgt)
        n_wgt = s_wgt.value

        pe.wait(s_const, n_const)
        dve.wait(s_const, n_const)
        act.wait(s_const, n_const)
        pe.wait(s_wgt, n_wgt)
        for srcv, dstv in ((w0[:, 0:P], w0a), (w0[:, P:2 * P], w0b), (wp[:, :], wpT), (wl[:, :], wlT), (wr[:, :], wrT)):
            pe.wait(s_prep, s_prep.value)
            n = pe.do(lambda e, srcv=srcv: e.transpose(ps_t[1][:, 0:P], srcv, ident[:, :]), s_prepT)
            dve.wait(s_prepT, n)
            dve.do(lambda e, dstv=dstv: e.tensor_copy(dstv[:, :], ps_t[1][:, 0:P]), s_prep)
        dve.wait(s_wgt, n_wgt)
        act.wait(s_wgt, n_wgt)
        n_w = dve.do(lambda e: e.tensor_scalar(w1neg[:, :], w1[:, :], -1.0, None, ALU.mult), s_prep)
        pe.wait(s_prep, n_w)

        node_bank = {"next": 0, "of": 6}
        h_ready = {}
        node_banks = ps[2:8]

        def next_bank():
            k = node_bank["next"] % node_bank["of"]
            node_bank["next"] += 1
            return node_banks[k], "bank%d" % k

        node_free = {}
        x_ready = {}

        def wait_free(q, key):
            for s, v in node_free.get(key, ()):
                q.wait(s, v)

        def layernorm(layer, i, c, m, res):
            if layer == 0:
                dve.wait(s_xin[i], s_xin[i].value)
                act.wait(s_xin[i], s_xin[i].value)
            dve.wait(s_node, x_ready.get(c, 0))
            for b in range(c, c + m):
                n = dve.do(lambda e, b=b: e.bn_stats(stats[:, b, :], x[:, b, :]), s_ln)
            dve.wait(s_ln, n)
            for b in range(c, c + m):
                n = dve.do(lambda e, b=b: e.bn_aggr(mv[:, b, :], stats[:, b, :]), s_ln)
            act.wait(s_ln, n)
            n_std = act.do(lambda e: e.activation(std[:, c:c + m], mv[:, c:c + m, 1], ACT.Sqrt, bias=eps_ln[:, 0:1]), s_sqrt)
            yield
            dve.wait(s_sqrt, n_std)
            n = dve.do(lambda e: e.reciprocal(rstd[:, c:c + m], std[:, c:c + m]), s_ln)
            dve.wait(s_ln, n)
            n = dve.do(lambda e: e.scalar_tensor_tensor(out=nmr[:, c:c + m], in0=mv[:, c:c + m, 0], scalar=-1.0,
                                                        in1=rstd[:, c:c + m], op0=ALU.mult, op1=ALU.mult), s_ln)
            act.wait(s_ln, n)
            act.wait(s_node, x_ready.get(c, 0))
            wait_free(act, "h%d" % c)
            for b in range(c, c + m):
                n = act.do(lambda e, b=b: e.activation(h[:, b, :], x[:, b, :], ACT.Relu, bias=nmr[:, b:b + 1],
                                                       scale=rstd[:, b:b + 1]), s_h)
            node_free["x%d" % c] = [(s_h, n)]
            res["h"] = n

        def transposed(blocks, ready, slot):
            bank = ps_t[slot]
            for s, v in ready:
                pe.wait(s, v)
            wait_free(pe, "ps_t%d" % slot)
            for j, blk in enumerate(blocks):
                f = lambda e, j=j, blk=blk: e.transpose(bank[:, j * P:(j + 1) * P], blk, ident[:, :])
                n = pe.do(f, s_tr) if j == len(blocks) - 1 else pe.do(f)
            act.wait(s_tr, n)
            wait_free(act, "hT%d" % slot)
            m = len(blocks)
            n = act.do(lambda e: e.copy(hT[:, slot, 0:m * P], bank[:, 0:m * P]), s_hT)
            node_free["ps_t%d" % slot] = [(s_hT, n)]
            return n

        def product(slot, m, weight, ready):
            bank, bank_key = next_bank()
            for s, v in ready:
                pe.wait(s, v)
            wait_free(pe, bank_key)
            for j in range(m):
                f = lambda e, j=j: e.matmul(bank[:, j * P:(j + 1) * P], hT[:, slot, j * P:(j + 1) * P], weight[:, :],
                                            start=True, stop=True)
                n = pe.do(f, s_mm) if j == m - 1 else pe.do(f)
            return bank[:, 0:m * P].rearrange("p (b f) -> p b f", f=P), n, bank_key

        def bcast(v, m):
            return v[:, :].unsqueeze(1).to_broadcast([P, m, P])

        def xadd(c, m, make):
            dve.wait(s_node, x_ready.get(c, 0))
            wait_free(dve, "x%d" % c)
            x_ready[c] = dve.do(make, s_node)
            return x_ready[c]

        tab_done = {}

        def table_write(make, s):
            n = sp.dma(make, s)
            tab_done[s] = n
            return n

        def rows_of(tab, c, m):
            return tab[c * P:(c + m) * P, :].rearrange("(b p) f -> p b f", p=P)

        def self_term(layer, i, c, m, slot, n_h, n_hT):
            xc = x[:, c:c + m, :]
            v, n, bank_key = product(slot, m, (w0a, w4, wrT, wloop)[layer], [(s_hT, n_hT)])
            node_free["hT%d" % slot] = [(s_mm, n)]
            yield
            dve.wait(s_mm, n)
            if layer == 0:
                n = xadd(c, m, lambda e: e.tensor_tensor(out=xc, in0=v, in1=xc, op=ALU.add))
                xadd(c, m, lambda e: e.tensor_tensor(out=xc, in0=xc, in1=bcast(bias0, m), op=ALU.add))
            elif layer == 1:
                tk = i % 4
                wait_free(dve, "tmp%d" % tk)
                n = dve.do(lambda e: e.tensor_tensor(out=tmp[:, tk, 0:m, :], in0=v, in1=bcast(bias4, m), op=ALU.add), s_node)
                dve.wait(s_node, n)
                dve.wait(s_node, x_ready.get(c, 0))
                wait_free(dve, "x%d" % c)
                for j in range(m):
                    nx = dve.do(lambda e, j=j: e.scalar_tensor_tensor(
                        out=x[:, c + j, :], in0=tmp[:, tk, j, :], scalar=indeg[:, c + j:c + j + 1],
                        in1=x[:, c + j, :], op0=ALU.mult, op1=ALU.add), s_node)
                x_ready[c] = nx
                node_free["tmp%d" % tk] = [(s_node, nx)]
            elif layer == 2:
                wait_free(dve, "sums%d" % c)
                n = dve.do(lambda e: e.tensor_tensor(out=rself[:, c:c + m, :], in0=v, in1=bcast(biasl, m), op=ALU.add), s_node)
            else:
                n = xadd(c, m, lambda e: e.tensor_tensor(out=xc, in0=v, in1=xc, op=ALU.add))
            node_free[bank_key] = [(s_node, n)]

        def node_pre(layer, i, c, m):
            res = {}
            yield from layernorm(layer, i, c, m, res)
            n_h = res["h"]
            slot = i % 2
            hc = h[:, c:c + m, :]
            if layer < 2:
                sp.wait(s_h, n_h)
                table_write(lambda e: e.dma_start(rows_of(tab_h[layer], c, m), hc), s_tabh)
            yield
            n_hT = transposed([h[:, b, :] for b in range(c, c + m)], [(s_h, n_h)], slot)
            node_free["h%d" % c] = [(s_tr, s_tr.value)]
            pe_ready = [(s_hT, n_hT)]
            yield
            if layer == 1:
                v, n, bank_key = product(slot, m, w1, pe_ready)
                yield
                act.wait(s_mm, n)
                wait_free(act, "stage%d" % slot)
                na = act.do(lambda e: e.copy(stage[:, slot, 0:m, :], v), s_relu)
                node_free[bank_key] = [(s_relu, na)]
                sp.wait(s_relu, na)
                nt_ = table_write(lambda e: e.dma_start(rows_of(tab_p, c, m), stage[:, slot, 0:m, :]), s_tab[slot])
                node_free["stage%d" % slot] = [(s_tab[slot], nt_)]
            elif layer == 2:
                v, n, bank_key = product(slot, m, wpT, pe_ready)
                dve.wait(s_h, n_h)
                n_xh = xadd(c, m, lambda e: e.tensor_tensor(out=x[:, c:c + m, :], in0=x[:, c:c + m, :], in1=hc, op=ALU.add))
                yield
                dve.wait(s_mm, n)
                wait_free(dve, "stage2%d" % slot)
                nd = dve.do(lambda e: e.tensor_tensor(out=stage2[:, slot, 0:m, :], in0=v, in1=bcast(biasp, m), op=ALU.add), s_node)
                node_free[bank_key] = [(s_node, nd)]
                act.wait(s_node, nd)
                assert nd > n_xh
                act.wait(s_tr, s_tr.value)
                na = act.do(lambda e: e.activation(hc, stage2[:, slot, 0:m, :], ACT.Relu), s_relu)
                node_free["stage2%d" % slot] = [(s_relu, na)]
                sp.wait(s_relu, na)
                table_write(lambda e: e.dma_start(rows_of(tab_m, c, m), hc), s_tabh)
            elif layer == 3:
                half = n_rel * P // 2
                rel_rows = tab_rel.rearrange("(n r) f -> n (r f)", r=n_rel)
                for j in range(m):
                    if j == 2:
                        yield
                    b = c + j
                    sl = b % 3
                    wait_free(act, "rel%d" % sl)
                    wait_free(dve, "rel%d" % sl)
                    for part in range(2):
                        bank, bank_key = next_bank()
                        pe.wait(s_hT, n_hT)
                        wait_free(pe, bank_key)
                        n = pe.do(lambda e, j=j, part=part, bank=bank: e.matmul(
                            bank[:, 0:half], hT[:, slot, j * P:(j + 1) * P], wrel[:, part * half:(part + 1) * half],
                            start=True, stop=True), s_mm)
                        dstv = stage_rel[:, sl, part * half:(part + 1) * half]
                        if part == 0:
                            act.wait(s_mm, n)
                            na = act.do(lambda e, bank=bank, dstv=dstv: e.copy(dstv, bank[:, 0:half]), s_relu)
                            node_free[bank_key] = [(s_relu, na)]
                        else:
                            dve.wait(s_mm, n)
                            nd = dve.do(lambda e, bank=bank, dstv=dstv: e.tensor_copy(dstv, bank[:, 0:half]), s_node)
                            node_free[bank_key] = [(s_node, nd)]
                    sp.wait(s_relu, na)
                    sp.wait(s_node, nd)
                    nt_ = table_write(lambda e, b=b, sl=sl: e.dma_start(rel_rows[b * P:(b + 1) * P, :], stage_rel[:, sl, :]), s_tab[sl])
                    node_free["rel%d" % sl] = [(s_tab[sl], nt_)]
            if layer == 3:
                node_free["hT%d" % slot] = [(s_mm, s_mm.value)]
                h_ready[c] = n_h
            else:
                yield from self_term(layer, i, c, m, slot, n_h, n_hT)

        def late_self_terms():
            for i, (c, m) in enumerate(chunks):
                slot = i % 2
                n_hT = transposed([h[:, b, :] for b in range(c, c + m)], [(s_h, h_ready[c])], slot)
                yield
                yield from self_term(3, i, c, m, slot, h_ready[c], n_hT)
                yield

        def node_sums(layer, c, m, ready):
            bank, bank_key = next_bank()
            for s, v in ready:
                pe.wait(s, v)
            wait_free(pe, bank_key)
            for j in range(m):
                f = lambda e, j=j: e.transpose(bank[:, j:j + 1], acc[0:1, 1, (c + j) * P:(c + j + 1) * P], ident[0:1, 0:1])
                n = pe.do(f, s_cnt) if j == m - 1 else pe.do(f)
            node_free["sums%d" % c] = [(s_cnt, n)]
            yield
            dve.wait(s_cnt, n)
            dst = (indeg, sumw)[layer]
            n = dve.do(lambda e: e.tensor_copy(dst[:, c:c + m], bank[:, 0:m]), s_node)
            node_free[bank_key] = [(s_node, n)]
            if layer == 0:
                dve.wait(s_node, n)
                n = dve.do(lambda e: e.tensor_scalar(rdeg[:, c:c + m], indeg[:, c:c + m], 1.0, None, ALU.max), s_node)
                dve.wait(s_node, n)
                n = dve.do(lambda e: e.reciprocal(rdeg[:, c:c + m], rdeg[:, c:c + m]), s_node)
            dve.wait(s_node, n)

        def node_post(layer, i, c, m, ready):
            xc = x[:, c:c + m, :]
            if layer < 2:
                yield from node_sums(layer, c, m, ready)
            cols = [acc[:, 0, b * P:(b + 1) * P] for b in range(c, c + m)]
            bank, bank_key = next_bank()
            for s, v in ready:
                pe.wait(s, v)
            wait_free(pe, bank_key)
            weight = {0: w0b, 2: wlT}.get(layer)
            for j in range(m):
                if weight is None:
                    f = lambda e, j=j: e.transpose(bank[:, j * P:(j + 1) * P], cols[j], ident[:, :])
                else:
                    f = lambda e, j=j: e.matmul(bank[:, j * P:(j + 1) * P], cols[j], weight[:, :], start=True, stop=True)
                n = pe.do(f, s_mm) if j == m - 1 else pe.do(f)
            v = bank[:, 0:m * P].rearrange("p (b f) -> p b f", f=P)
            if layer < 3:
                pool.wait(s_mm, n)
                pool.wait(s_cnt, s_cnt.value)
                halves = 2 if layer == 0 else 1
                pool.do(lambda e: e.memset(acc[:, 0:halves, c * P:(c + m) * P], 0.0), s_zero)
            yield
            dve.wait(s_mm, n)
            dve.wait(s_node, x_ready[c])
            if layer == 0:
                for j in range(m):
                    n = dve.do(lambda e, j=j: e.scalar_tensor_tensor(
                        out=x[:, c + j, :], in0=v[:, j, :], scalar=rdeg[:, c + j:c + j + 1], in1=x[:, c + j, :],
                        op0=ALU.mult, op1=ALU.add), s_node)
                x_ready[c] = n
                node_free[bank_key] = [(s_node, n)]
            elif layer == 1:
                for j in range(m):
                    n = dve.do(lambda e, j=j: e.scalar_tensor_tensor(
                        out=x[:, c + j, :], in0=h[:, c + j, :], scalar=sumw[:, c + j:c + j + 1], in1=x[:, c + j, :],
                        op0=ALU.mult, op1=ALU.add), s_node)
                x_ready[c] = n
                n = xadd(c, m, lambda e: e.tensor_tensor(out=xc, in0=xc, in1=v, op=ALU.subtract))
                node_free[bank_key] = [(s_node, n)]
                node_free["h%d" % c] = node_free["h%d" % c] + [(s_node, n)]
            elif layer == 2:
                tk = i % 4
                o, ex = rself[:, c:c + m, :], tmp[:, tk, 0:m, :]
                for j in range(m):
                    n = dve.do(lambda e, j=j: e.scalar_tensor_tensor(
                        out=o[:, j, :], in0=v[:, j, :], scalar=rdeg[:, c + j:c + j + 1], in1=o[:, j, :],
                        op0=ALU.mult, op1=ALU.add), s_node)
                node_free[bank_key] = [(s_node, n)]
                dve.wait(s_node, n)
                wait_free(dve, "tmp%d" % tk)
                n = dve.do(lambda e: e.tensor_scalar(ex, o, 0.0, None, ALU.min), s_node)
                nx = dve.do(lambda e: e.tensor_scalar(o, o, 0.0, None, ALU.max), s_node)
                act.wait(s_node, n)
                na = act.do(lambda e: e.activation(ex, ex, ACT.Exp), s_relu)
                yield
                dve.wait(s_node, nx)
                dve.wait(s_relu, na)
                nx = dve.do(lambda e: e.scalar_tensor_tensor(out=o, in0=ex, scalar=-1.0, in1=o, op0=ALU.add, op1=ALU.add), s_node)
                yield
                act.wait(s_node, nx)
                for j in range(m):
                    na = act.do(lambda e, j=j: e.activation(ex[:, j, :], o[:, j, :], ACT.Square,
                                                            accum_out=nrm[:, c + j:c + j + 1]), s_relu)
                node_free["tmp%d" % tk] = [(s_relu, na)]

            elif layer == 3:
                n = xadd(c, m, lambda e: e.tensor_tensor(out=xc, in0=v, in1=xc, op=ALU.add))
                node_free[bank_key] = [(s_node, n)]
                sp.wait(s_node, n)
                last = c + m == nb
                full = m - 1 if last else m
                if full:
                    sp.dma(lambda e: e.dma_start(out[c * P:(c + full) * P, :].rearrange("(b p) f -> p b f", p=P),
                                                 x[:, c:c + full, :]), s_out)
                if last:
                    sp.dma(lambda e: e.dma_start(out[(nb - 1) * P:n_nodes, :], x[0:last_rows, nb - 1, :]), s_out)

        slot_free = {}

        def edges(layer):
            table, idx = {0: (tab_h[0], idx_src), 1: (tab_h[1], idx_src),
                          2: (tab_m, idx_src), 3: (tab_rel, idx_rel)}[layer]
            for s, v in tab_done.items():
                pool.wait(s, v)
                if layer == 1:
                    sp.wait(s, v)
            tab_done.clear()
            g0 = 0 if layer in (1, 3) else npg
            tiles = [min(TPG, nt - g * TPG) for g in range(ng)]
            a_free = {}
            n_osum = {}
            n_row, n_one, n_scat, n_bc, n_pw, n_oneT, n_gT, n_exp, n_act, n_z, n_gate = ({} for _ in range(11))
            sums = 2 if layer < 2 else 1

            def gather(g):
                if g in n_row:
                    return
                sl = g % NSLOT
                for s, v in slot_free.get(sl, ()):
                    pool.wait(s, v)
                for t in range(tiles[g]):
                    col = g * TPG + t
                    n_row[g] = pool.dma(lambda e, t=t, col=col: e.indirect_dma_start(
                        out=rows[:, sl, t, :], out_offset=None, in_=table[:, :],
                        in_offset=bass.IndirectOffsetOnAxis(ap=idx[:, col:col + 1], axis=0)), s_row[sl])

            def onehot(g):
                sl, m = g % NONE, tiles[g]
                o = oneh[:, sl, 0:m, :]
                rel = dst_rel[:, g * TPG:g * TPG + m].unsqueeze(2).to_broadcast([P, m, WIN])
                if g - g0 >= NONE:
                    dve.wait(s_scat, n_scat[g - NONE])
                n = dve.do(lambda e: e.tensor_tensor(out=o, in0=iota_w.unsqueeze(1).to_broadcast([P, m, WIN]),
                                                     in1=rel, op=ALU.is_equal), s_one)
                if layer == 3:
                    dve.wait(s_one, n)
                    n = dve.do(lambda e: e.tensor_tensor(
                        out=o, in0=o, in1=wt[:, g * TPG:g * TPG + m].unsqueeze(2).to_broadcast([P, m, WIN]), op=ALU.mult), s_one)
                n_one[g] = n

            osum = onesumb if layer == 0 else onesum

            def sum_tiles(g):
                m = tiles[g]
                dve.wait(s_one, n_one[g])
                if g - g0 >= 2:
                    dve.wait(s_scat, n_scat[g - 2])

                def make(e):
                    with nc.allow_low_precision(reason="layer 0 sums at most four ones, exact in bfloat16"):
                        return e.tensor_reduce(out=osum[:, g % 2, :], in_=oneh[:, g % NONE, 0:m, :].rearrange("p t w -> p w t"),
                                               axis=AXX, op=ALU.add)
                n_osum[g] = dve.do(make, s_osum)

            def scatter(g):
                sl, m = g % NONE, tiles[g]
                bank = ps_a[g % 2]
                pe.wait(s_one, n_one[g])
                pe.wait(s_row[g % NSLOT], n_row[g])
                pe.wait(s_add, a_free.get(g % 2, 0))
                for t in range(m):
                    f = lambda e, t=t: e.matmul(bank[:, 0:WIN], rows[:, g % NSLOT, t, :], oneh[:, sl, t, :],
                                                start=t == 0, stop=t == m - 1)
                    last = sums == 1 and t == m - 1
                    n = pe.do(f, s_scat) if last else pe.do(f)
                if sums == 2:
                    pe.wait(s_osum, n_osum[g])
                    n = pe.do(lambda e: e.matmul(bank[:, WIN:2 * WIN], (onesb if layer == 0 else ones)[:, :], osum[:, g % 2, :],
                                                 start=True, stop=True), s_scat)
                n_scat[g] = n
                slot_free[g % NSLOT] = [(s_scat, n)]

            def add_window(s, n, g, w, v):
                dve.wait(s, n)
                if s_add.value:
                    dve.wait(s_add, s_add.value)

                def make(e):
                    start = e.value_load(base_int[0:1, g:g + 1], min_val=0, max_val=npad - WIN)
                    a = acc[:, 0:sums, bass.ds(start, w)]
                    return e.tensor_tensor(out=a, in0=a, in1=v, op=ALU.add)
                return dve.do(make, s_add)

            def accumulate(g):
                v = ps_a[g % 2][:, 0:sums * WIN].rearrange("p (k w) -> p k w", k=sums)
                a_free[g % 2] = add_window(s_scat, n_scat[g], g, WIN, v)

            def count_packs():
                tiles_of = [(k, t0 + j, j == 0, j == n_t - 1, w) for k, (t0, n_t, w) in enumerate(packs) for j in range(n_t)]
                n_pair, n_cnt, n_srow, n_cev, n_bank = {}, {}, {}, {}, {}
                lag = NQS - 1
                bundle_of = {k: (u, k - members[0]) for u, members in enumerate(bundles) for k in members}
                n_csum, n_pk, n_turn, n_added = {}, {}, {}, {}

                def compare(i):
                    k, t, _, _, w = tiles_of[i]
                    if i % TPG == 0:
                        q = i // TPG
                        if q >= 2:
                            dve.wait(s_count, n_cnt[i - TPG - 1])
                        n_srow[q] = dve.do(lambda e: e.tensor_tensor(
                            out=srow[:, q % 2, :, :], in0=iota_b[:, :].unsqueeze(1).to_broadcast([P, TPG, P]),
                            in1=src_row[:, t:t + TPG].unsqueeze(2).to_broadcast([P, TPG, P]), op=ALU.is_equal), s_srow)
                    pair = pairs[:, i % NQS, 0:nb * w]
                    on_act = i % 8 in ACT_TILES
                    if i >= NQS:
                        (act if on_act else dve).wait(s_count, n_cnt[i - NQS])
                    if on_act:
                        n = act.do(lambda e: e.activation(pair, iota_k[:, 0:nb * w], ACT.Square, bias=key[:, t:t + 1], scale=-1.0), s_paira)
                        act.wait(s_paira, n)
                        n_pair[i] = (s_paira, act.do(lambda e: e.activation(pair, pair, ACT.Relu, bias=ones[:, 0:1], scale=-1.0), s_paira))
                    else:
                        n_pair[i] = (s_pair, dve.do(lambda e: e.tensor_tensor(
                            out=pair, in0=iota_k[:, 0:nb * w], in1=key[:, t:t + 1].to_broadcast([P, nb * w]),
                            op=ALU.is_equal), s_pair))

                def count(i):
                    k, t, start, stop, w = tiles_of[i]
                    u, place = bundle_of[k]
                    per_bank = 512 // w
                    pe.wait(*n_pair[i])
                    pe.wait(s_srow, n_srow[i // TPG])
                    for b, q0 in enumerate(range(0, nb, per_bank)):
                        q1 = min(nb, q0 + per_bank)
                        if start:
                            pe.wait(s_cev, n_cev.get(b, 0))
                        f = lambda e, b=b, q0=q0, q1=q1: e.matmul(
                            ps[2 + b][:, 0:(q1 - q0) * w], srow[:, i // TPG % 2, i % TPG, :],
                            pairs[:, i % NQS, q0 * w:q1 * w], start=start, stop=stop)
                        if q1 == nb or stop:
                            n = pe.do(f, s_count)
                            n_bank[b] = n
                        else:
                            pe.do(f)
                    n_cnt[i] = n
                    if stop:
                        if u >= 1 and place == 0:
                            act.wait(s_pack, n_pk[u - 1])
                            if sums == 2:
                                act.wait(s_csum, n_csum[u - 1])
                        for b, q0 in enumerate(range(0, nb, per_bank)):
                            q1 = min(nb, q0 + per_bank)
                            act.wait(s_count, n_bank[b])
                            n_cev[b] = act.do(lambda e, b=b, q0=q0, q1=q1: e.copy(
                                counts[:, q0:q1, place * w:(place + 1) * w],
                                ps[2 + b][:, 0:(q1 - q0) * w].rearrange("p (q w) -> p q w", w=w)), s_cev)

                def multiply(u):
                    members = bundles[u]
                    w = packs[members[0]][2]
                    width = len(members) * w
                    if sums == 2:
                        dve.wait(s_cev, s_cev.value)
                        if u >= 1:
                            dve.wait(s_turn, n_turn[u - 1])
                        n_csum[u] = dve.do(lambda e: e.tensor_reduce(
                            out=csum[:, 0:width], in_=counts[:, :, 0:width].rearrange("p q w -> p w q"),
                            axis=AXX, op=ALU.add), s_csum)
                    pe.wait(s_cev, s_cev.value)
                    if u >= 1:
                        pe.wait(s_wev, n_wev[u - 1])
                    for q in range(nb):
                        f = lambda e, q=q: e.matmul(ps[0][0:width, 0:P], counts[:, q, 0:width], h[:, q, :],
                                                    start=q == 0, stop=q == nb - 1)
                        n = pe.do(f, s_pack) if q == nb - 1 else pe.do(f)
                        if q % 7 == 6:
                            yield
                    n_pk[u] = n
                    act.wait(s_pack, n)
                    if u >= 1:
                        act.wait(s_turn, n_turn[u - 1])
                    n_wev[u] = act.do(lambda e: e.copy(wsum[0:width, :], ps[0][0:width, 0:P]), s_wev)
                    yield
                    pe.wait(s_wev, n_wev[u])
                    if u >= 1:
                        pe.wait(s_add, n_added[u - 1])
                    n = pe.do(lambda e: e.transpose(ps[1][:, 0:width], wsum[0:width, :], ident[0:width, 0:width]), s_turn)
                    if sums == 2:
                        pe.wait(s_csum, n_csum[u])
                        n = pe.do(lambda e: e.matmul(ps[1][:, width:2 * width], ones[:, :], csum[:, 0:width],
                                                     start=True, stop=True), s_turn)
                    n_turn[u] = n
                    yield
                    for place, k in enumerate(members):
                        v = ps[1][:, 0:sums * width].rearrange("p (k w) -> p k w", k=sums)[:, :, place * w:(place + 1) * w]
                        n_added[u] = add_window(s_turn, n, packs[k][0] // TPG, w, v)

                n_wev = {}
                running = iter(())
                for i in range(npt + lag):
                    if i < npt:
                        compare(i)
                    if i >= lag:
                        k = tiles_of[i - lag][0]
                        count(i - lag)
                        next(running, None)
                        if tiles_of[i - lag][3] and k == bundles[bundle_of[k][0]][-1]:
                            for _ in running:
                                pass
                            running = multiply(bundle_of[k][0])
                            next(running, None)
                    yield tiles_of[min(i, npt - 1)][4]
                for _ in running:
                    yield 0

            def fetch_window(g):
                sl, m = g % 3, tiles[g]
                if g >= 3:
                    sp.wait(s_oneT, n_oneT[g - 3])
                    sp.wait(s_hid, n_exp[g - 3])
                n_bc[g] = sp.dma(lambda e: e.dma_start(
                    dst_bc[:, sl, 0:m * P], dst_flat[g * TPG * P:(g * TPG + m) * P].partition_broadcast(WIN)), s_bc[sl])

                def make(e):
                    start = e.value_load(base_int[0:1, g:g + 1], min_val=0, max_val=npad - WIN)
                    return e.dma_start(pwin[:, sl, :], tab_p[bass.ds(start, WIN), :])
                n_pw[g] = sp.dma(make, s_pw[sl])

            def onehot_t(g):
                m = tiles[g]
                dve.wait(s_bc[g % 3], n_bc[g])
                if g >= 2:
                    dve.wait(s_hid, n_exp[g - 2])
                n_oneT[g] = dve.do(lambda e: e.tensor_scalar(
                    onehT[:, g % 2, 0:m * P], dst_bc[:, g % 3, 0:m * P], win_node[0:WIN, g:g + 1], None, ALU.is_equal), s_oneT)

            def turn_rows(g):
                m, sl = tiles[g], g % 2
                pe.wait(s_row[g % NSLOT], n_row[g])
                if g >= 2:
                    pe.wait(s_gT, n_gT[g - 2])
                for t in range(m):
                    f = lambda e, t=t: e.transpose(ps_t[sl][:, t * P:(t + 1) * P], rows[:, g % NSLOT, t, :], ident[:, :])
                    n = pe.do(f, s_rowT) if t == m - 1 else pe.do(f)
                act.wait(s_rowT, n)
                if g >= 2:
                    act.wait(s_hid, n_exp[g - 2])
                n_gT[g] = act.do(lambda e: e.copy(hT[:, sl, 0:m * P], ps_t[sl][:, 0:m * P]), s_gT)

            def hidden(g):
                m, sl = tiles[g], g % 2
                v = ps_e[sl][:, 0:m * P]
                pe.wait(s_oneT, n_oneT[g])
                pe.wait(s_pw[g % 3], n_pw[g])
                if g >= 2:
                    pe.wait(s_act, n_act[g - 2])
                pe.do(lambda e: e.matmul(v, pwin[:, g % 3, :], onehT[:, sl, 0:m * P], start=True, stop=False))
                pe.wait(s_gT, n_gT[g])
                n_exp[g] = pe.do(lambda e: e.matmul(v, w1neg[:, :], hT[:, sl, 0:m * P], start=False, stop=True), s_hid)
                act.wait(s_hid, n_exp[g])
                if g >= 2:
                    act.wait(s_z, n_z[g - 2])
                n_act[g] = act.do(lambda e: e.activation(hid[:, sl, 0:m * P], v, ACT.Relu, bias=b1col[:, 0:1]), s_act)

            def gates(g):
                m, sl = tiles[g], g % 2
                pe.wait(s_act, n_act[g])
                if g >= 2:
                    pe.wait(s_gate, n_gate[g - 2])
                for t in range(m):
                    f = lambda e, t=t: e.matmul(ps_m[sl][:, t:t + 1], hid[:, sl, t * P:(t + 1) * P], w2col[:, :], start=True, stop=True)
                    n = pe.do(f, s_z) if t == m - 1 else pe.do(f)
                n_z[g] = n
                act.wait(s_z, n)
                if g >= 2:
                    act.wait(s_one, n_one2[g - 2])
                n_gate[g] = act.do(lambda e: e.activation(gate[:, sl, 0:m], ps_m[sl][:, 0:m], ACT.Sigmoid, bias=b2[:, 0:1]), s_gate)

            n_one2 = {}

            def weigh(g):
                m, sl = tiles[g], g % NONE
                dve.wait(s_gate, n_gate[g])
                dve.wait(s_one, n_one[g])
                o = oneh[:, sl, 0:m, :]
                n_one[g] = dve.do(lambda e: e.tensor_tensor(
                    out=o, in0=o, in1=gate[:, g % 2, 0:m].unsqueeze(2).to_broadcast([P, m, WIN]), op=ALU.mult), s_one)
                n_one2[g] = n_one[g]

            for k in range(len(node_banks)):
                wait_free(pe, "bank%d" % k)
            for k in range(2):
                wait_free(pe, "ps_t%d" % k)
                wait_free(act, "hT%d" % k)
            if layer == 0:
                for g in range(g0, min(g0 + 2, ng)):
                    gather(g)
                pool.do(lambda e: e.memset(acc[:, :, :], 0.0), s_zero)
            dve.wait(s_zero, s_zero.value)
            if layer in (1, 2):
                for q in (sp, act, dve):
                    q.wait(s_node, s_node.value)
                    q.wait(s_relu, s_relu.value)
            if layer != 1:
                steps = ((0, gather), (0, onehot)) + ((0, sum_tiles),) * (sums - 1) + ((1, accumulate), (0, scatter))
            else:
                steps = ((4, accumulate), (3, weigh), (3, sum_tiles), (3, scatter), (2, gates), (1, hidden),
                         (0, gather), (0, fetch_window), (0, turn_rows), (0, onehot_t), (2, onehot))
            turns = ng - g0 + max(behind for behind, _ in steps)
            pack_steps = count_packs() if g0 else iter(())
            if layer == 3:
                node_bank["of"] = 4
            self_steps = late_self_terms() if layer == 3 else iter(())
            per_turn, credit = PACK_LEAD * sum(n_t * w for _, n_t, w in packs) / (ng - g0), 0.0
            for turn in range(turns):
                for behind, step in steps:
                    if 0 <= turn - behind < ng - g0:
                        step(g0 + turn - behind)
                if turn % 4 == 3:
                    next(self_steps, None)
                credit += per_turn
                while g0 and credit > 0:
                    cost = next(pack_steps, None)
                    if cost is None:
                        break
                    credit -= cost
            for _ in pack_steps:
                pass
            for _ in self_steps:
                pass
            node_bank["of"] = 6
            if g0:
                for c, _ in chunks:
                    node_free["h%d" % c] = node_free.get("h%d" % c, []) + [(s_pack, s_pack.value)]
            general(layer, table, idx, sums, g0)

        def general(layer, table, idx, sums, g0):
            q = gen_sems[layer]
            rowbuf = rows[:, 0, :, :]
            one = rows[:, 1, :, :]
            p_dst = rows[:, 2, :, :]
            p_src = rows[:, 3, :, :]
            bank = ps_a[0]

            def guarded(body):
                def run(eng):
                    flag = eng.value_load(outside[0:1, 0:1], min_val=0, max_val=n_edges + npt * P)
                    with eng.If(flag):
                        body(eng)
                return run

            def on_dve(e):
                for lo, hi in ((0, g0), (g0, ng)):
                    if lo < hi:
                        groups_on_dve(e, lo, hi)

            def groups_on_dve(e, lo, hi):
                with e.Fori(lo, hi) as g:
                    cols = bass.ds(g * TPG, TPG)
                    rel = dst_rel[:, cols]
                    e.tensor_copy(gen_idx[:, :], idx[:, cols])
                    if layer == 3:
                        e.tensor_copy(gen_wt[:, :], wt[:, cols])
                    e.tensor_scalar(gen_in[:, :], key[:, cols] if hi == g0 else rel, 0.0, None, ALU.is_ge)
                    e.tensor_scalar(gen_abs[:, :], rel, win_node[:, bass.ds(g, 1)], None, ALU.add)
                    e.drain()
                    if hi != g0:
                        e.scalar_tensor_tensor(out=gen_in[:, :], in0=rel, scalar=float(WIN), in1=gen_in[:, :],
                                               op0=ALU.is_lt, op1=ALU.mult)
                    e.tensor_scalar(gen_abs[:, :], gen_abs[:, :], iota_p[:, 0:1], None, ALU.subtract)
                    e.drain()
                    e.scalar_tensor_tensor(out=gen_dst[:, :], in0=gen_in[:, :], scalar=-4.0 * npad, in1=gen_abs[:, :],
                                           op0=ALU.mult, op1=ALU.add)
                    e.tensor_scalar(gen_tgt[:, :], gen_abs[:, :], 0.0, None, ALU.max)
                    e.drain().then_inc(q["idx"], 1)
                    if layer == 1:
                        e.wait_ge(q["prow"], (g + 1) * (2 * 16 * TPG))
                        dd = p_dst
                        e.tensor_tensor(out=dd, in0=p_dst, in1=p_src, op=ALU.subtract)
                        e.drain()
                        e.tensor_tensor(out=dd, in0=dd, in1=bcast(bias1, TPG), op=ALU.add)
                        e.drain()
                        e.scalar_tensor_tensor(out=dd, in0=dd, scalar=0.0, in1=bcast(w2, TPG), op0=ALU.max, op1=ALU.mult)
                        e.drain()
                        e.tensor_reduce(out=zed[:, :], in_=dd, axis=AXX, op=ALU.add).then_inc(q["z"], 1)
                        e.wait_ge(q["gate"], g + 1)
                        e.tensor_copy(gen_wt[:, :], gate[:, 0, :])
                        e.drain()
                    with e.Fori(0, nb) as b:
                        done = g * nb + b
                        e.tensor_tensor(out=one, in0=iota_b[:, :].unsqueeze(1).to_broadcast([P, TPG, P]),
                                        in1=gen_dst[:, :].unsqueeze(2).to_broadcast([P, TPG, P]), op=ALU.is_equal)
                        e.drain()
                        e.tensor_scalar(gen_dst[:, :], gen_dst[:, :], float(P), None, ALU.subtract)
                        if layer in (1, 3):
                            e.tensor_tensor(out=one, in0=one, in1=gen_wt[:, :].unsqueeze(2).to_broadcast([P, TPG, P]),
                                            op=ALU.mult)
                        e.drain().then_inc(q["one"], 1)
                        e.wait_ge(q["scat"], done + 1)
                        a = acc[:, 0:sums, bass.ds(b * P, P)]
                        v = bank[:, 0:sums * P].rearrange("p (k w) -> p k w", k=sums)
                        e.tensor_tensor(out=a, in0=a, in1=v, op=ALU.add)
                        e.drain()

            def on_pool(e):
                with e.Fori(0, ng) as g:
                    e.wait_ge(q["idx"], g + 1)
                    e.sem_inc(q["seen"])
                    for t in range(TPG):
                        e.indirect_dma_start(out=rowbuf[:, t, :], out_offset=None, in_=table[:, :],
                                             in_offset=bass.IndirectOffsetOnAxis(ap=gen_idx[:, t:t + 1], axis=0)
                                             ).then_inc(q["row"], 16)
                    for buf, num in ((p_dst, gen_tgt), (p_src, gen_idx)) if layer == 1 else ():
                        for t in range(TPG):
                            e.indirect_dma_start(out=buf[:, t, :], out_offset=None, in_=tab_p[:, :],
                                                 in_offset=bass.IndirectOffsetOnAxis(ap=num[:, t:t + 1], axis=0)
                                                 ).then_inc(q["prow"], 16)

            def on_act(e):
                with e.Fori(0, ng) as g:
                    e.wait_ge(q["z"], g + 1)
                    e.activation(gate[:, 0, :], zed[:, :], ACT.Sigmoid, bias=b2[:, 0:1]).then_inc(q["gate"], 1)

            def on_pe(e):
                with e.Fori(0, ng) as g:
                    e.wait_ge(q["row"], (g + 1) * (16 * TPG))
                    e.sem_inc(q["seen"])
                    with e.Fori(0, nb) as b:
                        e.wait_ge(q["one"], g * nb + b + 1)
                        for t in range(TPG):
                            last = e.matmul(bank[:, 0:P], rowbuf[:, t, :], one[:, t, :], start=t == 0, stop=t == TPG - 1)
                        for t in range(TPG if sums == 2 else 0):
                            last = e.matmul(bank[:, P:2 * P], ones[:, :], one[:, t, :], start=t == 0, stop=t == TPG - 1)
                        last.then_inc(q["scat"], 1)

            dve.wait(s_add, s_add.value)
            dve.do(guarded(on_dve))
            pool.do(guarded(on_pool))
            pe.do(guarded(on_pe))
            if layer == 1:
                act.do(guarded(on_act))
            dve.do(lambda e: e.drain(), s_gen)

        def norm_scale(b0, b1):
            v = nrm[:, b0:b1]
            act.wait(s_relu, s_relu.value)
            na = act.do(lambda e: e.activation(v, v, ACT.Sqrt), s_relu)
            dve.wait(s_relu, na)
            n = dve.do(lambda e: e.tensor_scalar(v, v, EPS_NORM, None, ALU.max), s_node)
            dve.wait(s_node, n)
            n = dve.do(lambda e: e.reciprocal(v, v), s_node)
            dve.wait(s_node, n)

        def add_normed(c, m):
            dve.wait(s_node, x_ready[c])
            for j in range(m):
                n = dve.do(lambda e, j=j: e.scalar_tensor_tensor(
                    out=x[:, c + j, :], in0=rself[:, c + j, :], scalar=nrm[:, c + j:c + j + 1], in1=x[:, c + j, :],
                    op0=ALU.mult, op1=ALU.add), s_node)
            x_ready[c] = n

        def node_chunk(layer, i, c, m):
            if layer == 2:
                add_normed(c, m)
            else:
                yield from node_post(layer, i, c, m, [(s_add, s_add.value), (s_gen, s_gen.value)])
            if layer < 3:
                if layer == 2:
                    yield
                yield from node_pre(layer + 1, i, c, m)

        def rounds(chains):
            chains, running = list(chains), []
            while chains or running:
                if chains:
                    running.append(chains.pop(0))
                running = [r for r in running if next(r, "end") != "end"]
                yield

        def interleave(chains):
            for _ in rounds(chains):
                pass

        edge_tables = {}

        def prepare_edges():
            dve.wait(s_win, n_win)
            dve.do(lambda e: e.tensor_copy(f_src, raw_src), s_prep)
            n_dst = dve.do(lambda e: e.tensor_copy(f_dst, raw_dst), s_prep)
            n = dve.do(lambda e: e.tensor_copy(f_rel, raw_typ), s_prep)
            dve.wait(s_prep, n)
            n_flt = dve.do(lambda e: e.scalar_tensor_tensor(out=f_rel, in0=f_src, scalar=float(n_rel), in1=f_rel,
                                                            op0=ALU.mult, op1=ALU.add), s_prep)
            sp.wait(s_prep, n_dst)
            edge_tables["dstf"] = sp.dma(lambda e: e.dma_start(
                dst_flat.rearrange("(b p e) -> p b e", p=P, e=P), f_dst.rearrange("p (b e) -> p b e", e=P)), s_dstf)
            yield
            for srcv, dstv in ((f_dst, dst_rel), (f_src, idx_src), (f_rel, idx_rel), (raw_wt, wt)):
                for b0 in range(0, nr, CH):
                    m = min(CH, nr - b0)
                    bank, bank_key = next_bank()
                    pe.wait(s_prep, n_flt)
                    wait_free(pe, bank_key)
                    for j in range(m):
                        blk = srcv[:, (b0 + j) * P:(b0 + j + 1) * P]
                        f = lambda e, bank=bank, j=j, blk=blk: e.transpose(bank[:, j * P:(j + 1) * P], blk, ident[:, :])
                        n = pe.do(f, s_prepT) if j == m - 1 else pe.do(f)
                    dve.wait(s_prepT, n)
                    n = dve.do(lambda e, bank=bank, b0=b0, m=m, dstv=dstv: e.tensor_copy(
                        dstv[:, b0 * P:(b0 + m) * P], bank[:, 0:m * P]), s_prep)
                    node_free[bank_key] = [(s_prep, n)]
                    yield

        interleave([prepare_edges()] + [node_pre(0, i, c, m) for i, (c, m) in enumerate(chunks)])
        n_dstf = edge_tables["dstf"]
        wait_free(pe, "ps_t0")
        n_tab = s_prep.value
        dve.wait(s_prep, n_tab)
        first = dst_rel[0:1, 0:ng * TPG].rearrange("p (g t) -> p g t", t=TPG)[:, :, 0]
        dve.do(lambda e: e.tensor_scalar(base_row[:, :], first, float(npad - WIN), None, ALU.min), s_prep)
        dve.wait(s_prep, s_prep.value)
        n_base = dve.do(lambda e: e.tensor_copy(base_int[:, :], base_row[:, :]), s_prep)
        pe.wait(s_prep, n_base)
        n = pe.do(lambda e: e.matmul(ps_t[0][:, 0:ng], ones[0:1, :], base_row[:, :], start=True, stop=True), s_prepT)
        dve.wait(s_prepT, n)
        gd = dst_rel[:, 0:ng * TPG].rearrange("p (g t) -> p g t", t=TPG)
        n = dve.do(lambda e: e.tensor_tensor(out=gd, in0=gd, in1=ps_t[0][:, 0:ng].unsqueeze(2).to_broadcast([P, ng, TPG]),
                                         op=ALU.subtract), s_prep)
        n_prep = dve.do(lambda e: e.tensor_scalar(win_node[:, :], ps_t[0][:, 0:ng], iota_p[:, 0:1], None, ALU.add), s_prep)

        used = 4 * npt + ng * TPG
        assert used <= spare.shape[1]
        pool.wait(s_prep, n_prep)
        pool.wait(s_prepT, s_prepT.value)
        pool.wait(s_dstf, n_dstf)

        def step(make):
            dve.wait(s_prep, s_prep.value)
            dve.do(make, s_prep)

        u_blk, u_row = (spare[:, k * npt:(k + 1) * npt].bitcast(U32) for k in range(2))
        f_blk, f_in = (spare[:, k * npt:(k + 1) * npt] for k in (2, 3))
        pe_done = s_prepT.value
        dve.wait(s_prepT, pe_done)
        dve.wait(s_dstf, n_dstf)
        step(lambda e: e.tensor_scalar(u_blk, idx_src[:, 0:npt], 7, None, ALU.logical_shift_right))
        step(lambda e: e.tensor_scalar(u_row, idx_src[:, 0:npt], P - 1, None, ALU.bitwise_and))
        step(lambda e: e.tensor_copy(f_blk, u_blk))
        step(lambda e: e.tensor_copy(src_row[:, :], u_row))
        for t0, size, count, w in sections:
            if not count:
                continue
            a, b = t0, t0 + size * count
            kv = key[:, a:b].rearrange("p (g t) -> p g t", t=TPG)
            starts = win_node[:, a // TPG:b // TPG]
            step(lambda e, kv=kv, a=a, b=b, starts=starts: e.tensor_tensor(
                out=kv, in0=dst_rel[:, a:b].rearrange("p (g t) -> p g t", t=TPG),
                in1=starts.unsqueeze(2).to_broadcast([P, (b - a) // TPG, TPG]), op=ALU.add))
            kp = key[:, a:b].rearrange("p (k t) -> p k t", t=size)
            pack_start = starts.rearrange("p (k g) -> p k g", g=size // TPG)[:, :, 0]
            step(lambda e, kp=kp, pack_start=pack_start, count=count, size=size: e.tensor_tensor(
                out=kp, in0=kp, in1=pack_start.unsqueeze(2).to_broadcast([P, count, size]), op=ALU.subtract))
            kf, bf, nf = key[:, a:b], f_blk[:, a:b], f_in[:, a:b]
            step(lambda e, kf=kf, nf=nf: e.tensor_scalar(nf, kf, 0.0, None, ALU.is_ge))
            step(lambda e, kf=kf, nf=nf, w=w: e.scalar_tensor_tensor(out=nf, in0=kf, scalar=float(w), in1=nf, op0=ALU.is_lt, op1=ALU.mult))
            step(lambda e, kf=kf, bf=bf, w=w: e.scalar_tensor_tensor(out=kf, in0=bf, scalar=float(w), in1=kf, op0=ALU.mult, op1=ALU.add))
            step(lambda e, kf=kf, nf=nf: e.scalar_tensor_tensor(out=kf, in0=kf, scalar=1.0, in1=nf, op0=ALU.add, op1=ALU.mult))
            step(lambda e, kf=kf: e.tensor_scalar(kf, kf, 1.0, None, ALU.subtract))

        in_group = spare[:, 4 * npt:4 * npt + ng * TPG]
        gi = in_group.rearrange("p (g t) -> p g t", t=TPG)
        step(lambda e: e.tensor_scalar(gi, gd, 0.0, None, ALU.is_ge))
        step(lambda e: e.scalar_tensor_tensor(out=gi, in0=gd, scalar=float(WIN), in1=gi, op0=ALU.is_lt, op1=ALU.mult))
        step(lambda e: e.tensor_reduce(out=n_inside[:, :], in_=spare[:, 3 * npt:4 * npt + ng * TPG], axis=AXX, op=ALU.add))
        pe.wait(s_prep, s_prep.value)
        n = pe.do(lambda e: e.matmul(ps_t[0][:, 0:1], ones[:, :], n_inside[:, :], start=True, stop=True), s_prepT)
        dve.wait(s_prepT, n)
        dve.do(lambda e: e.tensor_scalar(outside[:, :], ps_t[0][0:1, 0:1], -1.0, float(n_edges + npt * P), ALU.mult, ALU.add), s_prep)

        n_prep = s_prep.value
        dve.wait(s_prep, n_prep)
        for q in (pe, sp, act):
            q.wait(s_prep, n_prep)
        sp.wait(s_dstf, n_dstf)
        node_free["ps_t0"] = node_free["ps_t1"] = [(s_prep, n_prep)]
        for slot in range(-(-used // (TPG * P))):
            slot_free[slot] = [(s_prep, n_prep)]
        for layer in range(4):
            edges(layer)
            numbered = [(i, c, m) for i, (c, m) in enumerate(chunks)]
            if layer != 2:
                interleave(node_chunk(layer, i, c, m) for i, c, m in numbered)
                continue
            ready = [(s_add, s_add.value), (s_gen, s_gen.value)]
            batches = [numbered[k:k + NORM_BATCH] for k in range(0, len(numbered), NORM_BATCH)]

            def to_h(batch, chains):
                yield from rounds(node_post(layer, i, c, m, ready) for i, c, m in batch)
                norm_scale(batch[0][1], batch[-1][1] + batch[-1][2])
                chains += [node_chunk(layer, i, c, m) for i, c, m in batch]
                for _ in range(STEPS_TO_H):
                    for chain in chains:
                        next(chain)
                    yield

            chains = []
            interleave([to_h(batches[0], chains)])
            for k in range(len(batches)):
                later = []
                ahead = to_h(batches[k + 1], later) if k + 1 < len(batches) else iter(())
                for _ in rounds(chains):
                    for _ in range(2):
                        next(ahead, None)
                interleave([ahead])
                chains = later
        sp.wait(s_out, s_out.value)

        block = ctx.enter_context(nc.Block())
        block.sync(lambda eng: sp.emit(eng))
        block.gpsimd(lambda eng: pool.emit(eng))
        block.scalar(lambda eng: act.emit(eng))
        block.vector(lambda eng: dve.emit(eng))
        block.tensor(lambda eng: pe.emit(eng))


_INS = ["x", "src", "dst", "edge_type_8", "edge_weight1", "L0_gnn_W", "L0_gnn_b", "L1_gnn_W1", "L1_gnn_b1",
        "L1_gnn_W2", "L1_gnn_b2", "L1_gnn_W4", "L1_gnn_b4", "L2_gnn_Wp", "L2_gnn_bp", "L2_gnn_Wl", "L2_gnn_bl",
        "L2_gnn_Wr", "L3_gnn_weight", "L3_gnn_loop_weight"]


def kernel(**inputs):
    import numpy as np
    import concourse.bacc as bacc
    from concourse.bass_utils import run_bass_kernel_spmd

    nc = bacc.Bacc("TRN2", target_bir_lowering=False, num_devices=1)
    arrays, args = {}, {}
    for name in _INS:
        a = np.ascontiguousarray(inputs[name])
        arrays["in_" + name] = a
        args[name] = nc.dram_tensor("in_" + name, a.shape, mybir.dt.from_np(a.dtype), kind="ExternalInput").ap()
    out = nc.dram_tensor("out_x", args["x"].shape, F32, kind="ExternalOutput").ap()
    gnn_program(nc, args, out)
    r = run_bass_kernel_spmd(nc, [arrays], core_ids=[0])
    return r.results[0]["out_x"]
```
